# Optimizing a Trainium2 kernel written in Bass

```python
import numpy as np
import jax
import jax.numpy as jnp

def _softmax(x, axis=-1):
    return jax.nn.softmax(x, axis=axis)

def _gelu(x):
    return jax.nn.gelu(x, approximate=True)

def _silu(x):
    return jax.nn.silu(x)

def _sigmoid(x):
    return jax.nn.sigmoid(x)

def _layernorm(x, axis=-1, eps=1e-05):
    m = jnp.mean(x, axis=axis, keepdims=True)
    v = jnp.var(x, axis=axis, keepdims=True)
    return (x - m) / jnp.sqrt(v + eps)

def _scatter_add(tgt, idx, src, axis=0):
    return tgt.at[idx].add(src)

def _segment_sum(src, seg, n):
    return jax.ops.segment_sum(src, seg, n)
kernel_name = 'mk_xattn_seq_d1_seqx_r2_aae670'

def setup_inputs(seed: int=0):
    np.random.seed(seed)
    _w = jnp.asarray

    def _rec_inputs():
        import jax
        import jax.numpy as jnp
        _rk = jax.random.key(seed)
        x = -0.000125 + 0.9999 * jax.random.normal(jax.random.fold_in(_rk, 1), (8, 100, 1024), jnp.float32)
        _lenS = 100 - jax.random.randint(jax.random.fold_in(_rk, 7), (8,), 0, max(1, 100 // 4) + 1, jnp.int32)
        _lenS2 = 722 - jax.random.randint(jax.random.fold_in(_rk, 8), (8,), 0, max(1, 722 // 4) + 1, jnp.int32)
        _ctx_1024P = jax.random.normal(jax.random.fold_in(_rk, 11), (8, 16, 512), jnp.float32)
        _ctx_1024c = jax.random.dirichlet(jax.random.fold_in(_rk, 511), 0.3 * jnp.ones((16,), jnp.float32), (8, 722))
        _ctx_1024t = jnp.einsum('bsk,bkd->bsd', _ctx_1024c, _ctx_1024P)
        _ctx_1024t = _ctx_1024t * jax.lax.rsqrt(jnp.mean(jnp.square(_ctx_1024t)) + 1e-12) * 0.953939
        ctx_1024 = 4.13588e-05 + 0.999923 * (_ctx_1024t + 0.3 * jax.random.normal(jax.random.fold_in(_rk, 611), (8, 722, 512), jnp.float32))
        return (x, ctx_1024)
    x, ctx_1024 = _rec_inputs()

    def _L0_xattn_setup():
        import jax, jax.numpy as jnp
        import numpy as np
        EPS = 1e-06

        def _rmsnorm(x, w):
            var = jnp.mean(jnp.square(x), axis=-1, keepdims=True)
            return x * jax.lax.rsqrt(var + EPS) * w
        key = jax.random.key(seed)
        ks = jax.random.split(key, 6)
        B, N, M = (4, 2048, 1024)
        d_model, memory_dim = (1024, 512)
        hidden_states = jax.random.normal(ks[0], (B, N, d_model), dtype=jnp.float32)
        memory = jax.random.normal(ks[1], (B, M, memory_dim), dtype=jnp.float32)
        W_mem = jax.random.normal(ks[2], (d_model, memory_dim), dtype=jnp.float32) / np.sqrt(memory_dim)
        W_gate = jax.random.normal(ks[3], (d_model, 2 * d_model), dtype=jnp.float32) / np.sqrt(2 * d_model)
        b_gate = jax.random.normal(ks[4], (d_model,), dtype=jnp.float32) * 0.01
        norm_w = jnp.ones((d_model,), dtype=jnp.float32)
        return {'hidden_states': hidden_states, 'memory': memory, 'W_mem': W_mem, 'W_gate': W_gate, 'b_gate': b_gate, 'norm_w': norm_w}
    _L0_xattn_all = _L0_xattn_setup()
    _L0_xattn_in = {k: v for k, v in _L0_xattn_all.items() if k in ('W_mem', 'W_gate', 'b_gate', 'norm_w')}
    del _L0_xattn_all
    return {'x': x, 'ctx_1024': ctx_1024, 'L0_xattn_W_mem': _L0_xattn_in['W_mem'], 'L0_xattn_W_gate': _L0_xattn_in['W_gate'], 'L0_xattn_b_gate': _L0_xattn_in['b_gate'], 'L0_xattn_norm_w': _L0_xattn_in['norm_w']}

def reference(x, ctx_1024, L0_xattn_W_mem, L0_xattn_W_gate, L0_xattn_b_gate, L0_xattn_norm_w):
    import jax
    import jax.numpy as jnp

    def _L0_xattn_ref(hidden_states, memory, W_mem, W_gate, b_gate, norm_w):
        import jax, jax.numpy as jnp
        import numpy as np
        EPS = 1e-06

        def _rmsnorm(x, w):
            var = jnp.mean(jnp.square(x), axis=-1, keepdims=True)
            return x * jax.lax.rsqrt(var + EPS) * w
        D = hidden_states.shape[-1]
        memory_proj = jnp.einsum('bme,de->bmd', memory, W_mem)
        scores = jnp.einsum('bnd,bmd->bnm', hidden_states, memory_proj) / jnp.sqrt(jnp.float32(D))
        attn = jax.nn.softmax(scores, axis=-1)
        memory_context = jnp.einsum('bnm,bmd->bnd', attn, memory_proj)
        gate_input = jnp.concatenate([hidden_states, memory_context], axis=-1)
        gate = jax.nn.sigmoid(jnp.einsum('bnf,df->bnd', gate_input, W_gate) + b_gate)
        fused = hidden_states + gate * memory_context
        return _rmsnorm(fused, norm_w)
    x = _L0_xattn_ref(x, ctx_1024, L0_xattn_W_mem, L0_xattn_W_gate, L0_xattn_b_gate, L0_xattn_norm_w)
    return x

_drawn_inputs = setup_inputs


def setup_inputs(seed=0):
    import zlib

    import numpy as np

    out = dict(_drawn_inputs(seed))
    spreads = {'L0_xattn_norm_w': (1.0, 0.2)}
    factors = {'L0_xattn_b_gate': 50.344}
    for name, (base, spread) in spreads.items():
        noise = np.random.default_rng([zlib.crc32(name.encode()), seed]).standard_normal(out[name].shape)
        drawn = base * np.exp(spread * noise) if base else spread * noise
        out[name] = jnp.asarray(drawn.astype(out[name].dtype))
    for name, factor in factors.items():
        out[name] = (out[name] * factor).astype(out[name].dtype)
    return out
```

```python
from contextlib import ExitStack

import concourse.bass as bass
from concourse import mybir

B, N, D = 8, 100, 1024
M, C = 722, 512
P = 128
R = B * N
H = R // 2
KD, KC = D // P, C // P
MT = M // P
ML = M - MT * P
MH = M // 2
BANK = 512
WB = KD * P
EPS = 1e-6

J_MEM = 0
J_GX = J_MEM + KD // 2
J_MC = J_GX + KD
J_G2 = J_MC + KD // 2
STEPS = 2 * KD


def build(nc, xT, ctxT, ctxN, w_mem, w_gate_x, w_mem_t, w_gate_mc, b_gate, norm_w, outT):
    F32, F32R = mybir.dt.float32, mybir.dt.float32r
    ALU, ACT, AX = mybir.AluOpType, mybir.ActivationFunctionType, mybir.AxisListType

    top = ExitStack()
    with top:
        def sb(scope, name, shape, dt=F32):
            return scope.enter_context(nc.sbuf_tensor(name, shape, dt))

        def sem(name):
            return top.enter_context(nc.semaphore(name))

        act_hi = sb(top, "act_hi", [P, KD, R], F32R)
        act_lo = sb(top, "act_lo", [P, KD, R], F32R)
        q_hi = sb(top, "q_hi", [P, KC, R], F32R)
        q_lo = sb(top, "q_lo", [P, KC, R], F32R)
        acc = sb(top, "acc", [P, KD, R])
        w_stage = sb(top, "w_stage", [P, 2, WB])
        w_hi = [sb(top, f"w_hi{i}", [P, WB], F32R) for i in range(2)]
        w_lo = [sb(top, f"w_lo{i}", [P, WB], F32R) for i in range(2)]
        ident = sb(top, "ident", [N, N])
        bias_t = sb(top, "bias_t", [P, KD])
        norm_t = sb(top, "norm_t", [P, KD])
        eps_t = sb(top, "eps_t", [P, 1])
        top_score = sb(top, "top_score", [N, 1])
        neg_top = sb(top, "neg_top", [N, 1])
        row_sum = sb(top, "row_sum", [N, 1])
        row_inv = sb(top, "row_inv", [N, 1])

        with ExitStack() as attn:
            ct_stage = sb(attn, "ct_stage", [P, KC, M])
            cn_stage = sb(attn, "cn_stage", [P, MT + 1, C])
            ct_hi = sb(attn, "ct_hi", [P, KC, M], F32R)
            ct_lo = sb(attn, "ct_lo", [P, KC, M], F32R)
            cn_hi = sb(attn, "cn_hi", [P, MT + 1, C], F32R)
            cn_lo = sb(attn, "cn_lo", [P, MT + 1, C], F32R)
            qb_hi = sb(attn, "qb_hi", [P, KC, N], F32R)
            qb_lo = sb(attn, "qb_lo", [P, KC, N], F32R)
            probs = sb(attn, "probs", [N, M])
            pt_hi = sb(attn, "pt_hi", [P, MT + 1, N], F32R)
            pt_lo = sb(attn, "pt_lo", [P, MT + 1, N], F32R)
            pc = sb(attn, "pc", [N, C])
        mc = sb(top, "mc", [P, KD, R])
        x_again = sb(top, "x_again", [P, KD, R])
        gate = sb(top, "gate", [P, 2, H])
        square = sb(top, "square", [P, 2, H])
        square_sum = sb(top, "square_sum", [P, 2, H])
        rms_inv = sb(top, "rms_inv", [P, 2, H])
        mean_w = sb(top, "mean_w", [P, P])

        ps = top.enter_context(nc.psum_tensor("ps", [P, 8 * BANK], F32))

        def bank(i, cols, rows=P, at=0):
            return ps[0:rows, i * BANK + at:i * BANK + at + cols]

        scores = ps[0:N, 0:2 * (BANK + 1)].rearrange("p (h m) -> p h m", h=2)[:, :, 0:MH]
        GXB, PTB, PTB5, PCB = 2, 4, 5, 6
        G2B, MSB = 4, 6
        gx_ps = ps[:, GXB * BANK:(GXB + 2) * BANK].rearrange("p (h m) -> p h m", h=2)[:, :, 0:H]

        x_in = [sem(f"x_in{k}") for k in range(KD)]
        w_in = [sem(f"w_in{s}") for s in range(2)]
        ct_in = [sem(f"ct_in{s}") for s in range(2)]
        cn_in = [sem(f"cn_in{s}") for s in range(2)]
        const_in = sem("const_in")
        xa_in = sem("xa_in")
        stored = sem("stored")
        x_hi_done, x_lo_done = sem("x_hi_done"), sem("x_lo_done")
        w_hi_done, w_lo_done = sem("w_hi_done"), sem("w_lo_done")
        ct_hi_done, ct_lo_done = sem("ct_hi_done"), sem("ct_lo_done")
        cn_hi_done, cn_lo_done = sem("cn_hi_done"), sem("cn_lo_done")
        q_hi_done, q_lo_done = sem("q_hi_done"), sem("q_lo_done")
        pt_hi_done, pt_lo_done = sem("pt_hi_done"), sem("pt_lo_done")
        at_hi_done, at_lo_done = sem("at_hi_done"), sem("at_lo_done")
        mc_lo_done = sem("mc_lo_done")
        w_used = sem("w_used")
        q_made = sem("q_made")
        scores_made = sem("scores_made")
        probsT_made = sem("probsT_made")
        pc_made = sem("pc_made")
        pcT_made = sem("pcT_made")
        mc_made = sem("mc_made")
        gate_made = sem("gate_made")
        mean_made = sem("mean_made")
        consts_set, eps_set = sem("consts_set"), sem("eps_set")
        ident_zeroed = sem("ident_zeroed")
        qb_copied = sem("qb_copied")
        top_found, neg_top_set = sem("top_found"), sem("neg_top_set")
        exp_done = sem("exp_done")
        inv_set = sem("inv_set")
        pc_scaled = sem("pc_scaled")
        gx_saved = sem("gx_saved")
        mc_saved = sem("mc_saved")
        gate_summed = sem("gate_summed")
        gate_done = sem("gate_done")
        gated, fused = sem("gated"), sem("fused")
        squared, weighted = sem("squared"), sem("weighted")
        summed = sem("summed")
        root_done, inv_done = sem("root_done"), sem("inv_done")
        mean_w_set = sem("mean_w_set")
        out0_done, out1_done = sem("out0_done"), sem("out1_done")

        ct_rows = ctxT.rearrange("b c m -> (b c) m")
        cn_rows = ctxN.rearrange("b m c -> (b m) c")
        wgx_rows = w_gate_x.rearrange("t p n -> (t p) n")
        wg2_rows = w_gate_mc.rearrange("t p n -> (t p) n")

        block = top.enter_context(nc.Block())

        @block.sync
        def _(sp):
            def load_x(k):
                sp.dma_start(acc[:, k, :], xT[k * P:(k + 1) * P, :]).then_inc(x_in[k], 16)

            def load_w(j, src, slot):
                if not isinstance(j, int) or j >= 2:
                    sp.wait_ge(w_lo_done, j - 1)
                sp.dma_start(w_stage[:, slot, :], src).then_inc(w_in[slot], 16)

            def load_ctxT(b, first=False):
                for s in range(2):
                    if not first:
                        sp.wait_ge(ct_lo_done, 2 * b - 1 + s)
                    sp.dma_start(ct_stage[:, 2 * s:2 * s + 2, :],
                                 ct_rows[bass.ds(b * C + s * 2 * P, 2 * P), :]
                                 .rearrange("(k p) m -> p k m", p=P)).then_inc(ct_in[s], 16)

            def load_ctx(b, first=False):
                if not first:
                    sp.wait_ge(cn_lo_done, 2 * b - 1)
                sp.dma_start(cn_stage[:, 0:3, :], cn_rows[bass.ds(b * M, 3 * P), :]
                             .rearrange("(t p) c -> p t c", p=P)).then_inc(cn_in[0], 16)
                if not first:
                    sp.wait_ge(cn_lo_done, 2 * b)
                sp.dma_start(cn_stage[:, 3:MT, :], cn_rows[bass.ds(b * M + 3 * P, (MT - 3) * P), :]
                             .rearrange("(t p) c -> p t c", p=P)).then_inc(cn_in[1], 16)
                sp.dma_start(cn_stage[0:ML, MT, :],
                             cn_rows[bass.ds(b * M + MT * P, ML), :]).then_inc(cn_in[1], 16)

            load_x(0)
            load_w(0, w_mem[0], 0)
            load_x(1)
            load_x(2)
            load_w(1, w_mem[1], 1)
            load_x(3)
            load_x(4)
            load_x(5)
            load_w(2, w_mem[2], 0)
            load_x(6)
            load_x(7)
            load_w(3, w_mem[3], 1)
            load_ctxT(0, first=True)
            load_ctx(0, first=True)
            sp.dma_start(bias_t[:, :], b_gate).then_inc(const_in, 16)
            sp.dma_start(norm_t[:, :], norm_w).then_inc(const_in, 16)
            load_w(J_GX, w_gate_x[0], 0)
            load_w(J_GX + 1, w_gate_x[1], 1)

            def ahead(b, slot):
                load_w(J_GX + 2 + b, wgx_rows[bass.ds((b + 2) * P, P), :], slot)
                load_ctxT(b + 1)
                load_ctx(b + 1)

            with sp.Fori(0, B // 2 - 1) as i:
                b = 2 * i
                ahead(b, 0)
                ahead(b + 1, 1)
            load_w(J_MC, w_mem_t[0], 0)
            load_ctxT(B - 1)
            load_ctx(B - 1)
            load_w(J_MC + 1, w_mem_t[1], 1)
            load_w(J_MC + 2, w_mem_t[2], 0)
            load_w(J_MC + 3, w_mem_t[3], 1)
            load_w(J_G2, w_gate_mc[0], 0)

            sp.wait_ge(mc_made, 1)
            sp.dma_start(x_again[:, :, :], xT.rearrange("(k p) r -> p k r", p=P)).then_inc(xa_in, 16)
            load_w(J_G2 + 1, w_gate_mc[1], 1)
            with sp.Fori(0, KD // 2 - 1) as i:
                for u in range(2):
                    load_w(J_G2 + 2 + 2 * i + u, wg2_rows[bass.ds((2 * i + u + 2) * P, P), :], u)
            with sp.Fori(0, KD // 2) as i:
                for u in range(2):
                    load_w(J_G2 + KD + 2 * i + u, wg2_rows[bass.ds((2 * i + u) * P, P), :], u)
            out_v = outT.rearrange("(k p) r -> p k r", p=P)
            sp.wait_ge(out0_done, KD)
            sp.dma_start(out_v[:, :, 0:H], acc[:, :, 0:H]).then_inc(stored, 16)
            for k in range(KD):
                sp.wait_ge(out1_done, k + 1)
                sp.dma_start(out_v[:, k, H:R], acc[:, k, H:R]).then_inc(stored, 16)
            sp.wait_ge(stored, 16 * (KD + 1))

        @block.tensor
        def _(pe):
            def three(outs, weight, stream, first, last):
                (wh, wl), done = weight, None
                for wgt, part in ((wh, 0), (wh, 1), (wl, 0)):
                    for h, o in enumerate(outs):
                        done = nc.tensor.matmul(o, wgt, stream[h][part],
                                                start=first and wgt is wh and part == 0,
                                                stop=last and wgt is wl)
                return done

            def w_tile(slot, i):
                return w_hi[slot][:, i * P:(i + 1) * P], w_lo[slot][:, i * P:(i + 1) * P]

            def halves(hi, lo, k):
                return [(hi[:, k, h * H:(h + 1) * H], lo[:, k, h * H:(h + 1) * H]) for h in range(2)]

            for k in range(KD):
                if k % 2 == 0:
                    pe.wait_ge(w_lo_done, k // 2 + 1)
                pe.wait_ge(x_lo_done, k + 1)
                last_k = k == KD - 1
                if not last_k:
                    for c in range(KC):
                        done = three([bank(c, H), bank(c + 4, H)], w_tile(k // 2 % 2, k % 2 * 4 + c),
                                     halves(act_hi, act_lo, k), k == 0, False)
                else:
                    for h in range(2):
                        for c in range(KC):
                            done = three([bank(c + 4 * h, H)], w_tile(k // 2 % 2, k % 2 * 4 + c),
                                         halves(act_hi, act_lo, k)[h:h + 1], False, True)
                            if (h, c) != (1, KC - 1):
                                done.then_inc(q_made, 1)
                if k % 2 == 1:
                    done.then_inc(w_used, 1)

            def gate_x(slot, k0, k1):
                for k in range(k0, k1):
                    last = three([bank(GXB, H), bank(GXB + 1, H)], w_tile(slot, k),
                                 halves(act_hi, act_lo, k), k == 0, k == KD - 1)
                return last

            def step(b, slot, cuts):
                def fill(i):
                    return gate_x(slot, cuts[i], cuts[i + 1])

                if cuts[1] > 0:
                    pe.wait_ge(w_lo_done, J_GX + 1 + b)
                    fill(0)
                pe.wait_ge(ct_lo_done, 2 * b + 2)
                pe.wait_ge(qb_copied, b + 1)
                for k in range(KC):
                    for lhs, rhs, part in ((qb_hi, ct_hi, 0), (qb_hi, ct_lo, 1), (qb_lo, ct_hi, 2)):
                        for h in range(2):
                            at = h * (MH - 1)
                            done = nc.tensor.matmul(bank(h, MH + 1, N), lhs[:, k, :],
                                                    rhs[:, k, at:at + MH + 1],
                                                    start=k == 0 and part == 0,
                                                    stop=k == KC - 1 and part == 2)
                done.then_inc(scores_made, 1)
                if cuts[1] == 0:
                    pe.wait_ge(w_lo_done, J_GX + 1 + b)
                    pe.wait_ge(gx_saved, 2 * b)
                fill(1)
                pe.wait_ge(exp_done, b + 1)
                for t in range(MT + 1):
                    rows = P if t < MT else ML
                    o = bank(PTB, N, P, t * N) if t < MT else bank(PTB5, N, ML, KC * N)
                    done = nc.tensor.transpose(o, probs[:, t * P:t * P + rows], ident[:, :])
                done.then_inc(probsT_made, 1)
                fill(2)
                pe.wait_ge(pt_lo_done, b + 1)
                pe.wait_ge(cn_lo_done, 2 * b + 2)
                for t in range(MT + 1):
                    rows = P if t < MT else ML
                    for lhs, rhs, part in ((pt_hi, cn_hi, 0), (pt_hi, cn_lo, 1), (pt_lo, cn_hi, 2)):
                        done = nc.tensor.matmul(bank(PCB, C, N), lhs[0:rows, t, :], rhs[0:rows, t, :],
                                                start=t == 0 and part == 0, stop=t == MT and part == 2)
                done.then_inc(pc_made, 1)
                fill(3)
                pe.wait_ge(pc_scaled, b + 1)
                for c in range(KC):
                    done = nc.tensor.transpose(bank(PTB5, N, P, c * N), pc[:, c * P:(c + 1) * P],
                                               ident[:, :])
                done.then_inc(pcT_made, 1)
                fill(4).then_inc(w_used, 1)

            pe.wait_ge(consts_set, 1)
            pe.wait_ge(q_lo_done, KC)
            step(0, 0, (0, 3, 5, 6, 7, KD))
            CUTS = (0, 0, 3, 5, 7, KD)
            step(1, 1, CUTS)
            with pe.Fori(1, B // 2) as i:
                step(2 * i, 0, CUTS)
                step(2 * i + 1, 1, CUTS)

            pe.wait_ge(at_lo_done, B)
            pe.wait_ge(gx_saved, 2 * B)

            def mc_block(q, slot, free):
                pe.wait_ge(w_lo_done, J_MC + 1 + q)
                for u in range(2):
                    if free:
                        pe.wait_ge(mc_saved, 2 * q + u - 1)
                    for k in range(KC):
                        done = three([bank(2 * u, H), bank(2 * u + 1, H)], w_tile(slot, u * KC + k),
                                     halves(q_hi, q_lo, k), k == 0, k == KC - 1)
                    done.then_inc(mc_made, 1)

            mc_block(0, 0, False)
            mc_block(1, 1, True)
            mc_block(2, 0, True)
            mc_block(3, 1, True)

            def gate_mc(t, h, slot, free):
                pe.wait_ge(w_lo_done, J_G2 + 1 + t)
                if free:
                    pe.wait_ge(gate_summed, t - 1)
                for k in range(KD):
                    if not free and slot == 0:
                        pe.wait_ge(mc_lo_done, k + 1)
                    done = three([bank(G2B + slot, H)], w_tile(slot, k),
                                 halves(act_hi, act_lo, k)[h:h + 1], k == 0, k == KD - 1)
                done.then_inc(gate_made, 1)

            def mean_square(h):
                pe.wait_ge(summed, KD * (h + 1))
                nc.tensor.matmul(bank(MSB, H), mean_w[:, :], square_sum[:, h, :],
                                 start=True, stop=True).then_inc(mean_made, 1)

            gate_mc(0, 0, 0, False)
            gate_mc(1, 0, 1, False)
            with pe.Fori(1, KD // 2) as i:
                t = 2 * i
                gate_mc(t, 0, 0, True)
                gate_mc(t + 1, 0, 1, True)
            gate_mc(KD, 1, 0, True)
            gate_mc(KD + 1, 1, 1, True)
            mean_square(0)
            with pe.Fori(KD // 2 + 1, STEPS // 2) as i:
                t = 2 * i
                gate_mc(t, 1, 0, True)
                gate_mc(t + 1, 1, 1, True)
            mean_square(1)

        @block.scalar
        def _(act):
            def split_w(j, slot, free=None):
                act.wait_ge(w_in[slot], 8 * (j - slot) + 16)
                if free is not None:
                    act.wait_ge(*free)
                elif not isinstance(j, int) or j >= 2:
                    act.wait_ge(w_used, j - 1)
                nc.scalar.activation(w_hi[slot][:, :], w_stage[:, slot, :], ACT.Copy).then_inc(w_hi_done, 1)

            def split_x(k):
                act.wait_ge(x_in[k], 16)
                nc.scalar.activation(act_hi[:, k, :], acc[:, k, :], ACT.Copy).then_inc(x_hi_done, 1)

            def split_ctxT(b):
                if not isinstance(b, int) or b > 0:
                    act.wait_ge(scores_made, b)
                for s in range(2):
                    act.wait_ge(ct_in[s], 16 * b + 16)
                    nc.scalar.activation(ct_hi[:, 2 * s:2 * s + 2, :], ct_stage[:, 2 * s:2 * s + 2, :],
                                         ACT.Copy).then_inc(ct_hi_done, 1)

            def split_ctx(b):
                if not isinstance(b, int) or b > 0:
                    act.wait_ge(pc_made, b)
                act.wait_ge(cn_in[0], 16 * b + 16)
                nc.scalar.activation(cn_hi[:, 0:3, :], cn_stage[:, 0:3, :], ACT.Copy).then_inc(cn_hi_done, 1)
                act.wait_ge(cn_in[1], 32 * b + 32)
                nc.scalar.activation(cn_hi[:, 3:MT, :], cn_stage[:, 3:MT, :], ACT.Copy)
                nc.scalar.activation(cn_hi[0:ML, MT, :], cn_stage[0:ML, MT, :], ACT.Copy).then_inc(cn_hi_done, 1)

            split_x(0)
            split_w(0, 0)
            split_x(1)
            split_x(2)
            split_w(1, 1)
            split_x(3)
            split_x(4)
            split_w(2, 0)
            split_x(5)
            split_x(6)
            split_x(7)
            split_w(3, 1)
            split_ctxT(0)
            split_ctx(0)
            split_w(J_GX, 0)
            for h in range(2):
                for c in range(KC):
                    if (h, c) != (1, KC - 1):
                        act.wait_ge(q_made, h * KC + c + 1)
                    else:
                        act.wait_ge(w_used, KD // 2)
                    nc.scalar.activation(q_hi[:, c, h * H:(h + 1) * H], bank(c + 4 * h, H),
                                         ACT.Copy).then_inc(q_hi_done, 1)

            def step(b, slot, more):
                act.wait_ge(neg_top_set, b + 1)
                nc.scalar.activation(probs[:, :].rearrange("p (h m) -> p h m", h=2), scores, ACT.Exp,
                                     bias=neg_top[:, :], scale=float(D) ** -0.5,
                                     accum_out=row_sum[:, :]).then_inc(exp_done, 1)
                split_w(J_GX + 1 + b, 1 - slot)
                act.wait_ge(probsT_made, b + 1)
                nc.scalar.activation(pt_hi[:, 0:MT, :], bank(PTB, MT * N).rearrange("p (t n) -> p t n", n=N),
                                     ACT.Copy)
                nc.scalar.activation(pt_hi[0:ML, MT, :], bank(PTB5, N, ML, KC * N), ACT.Copy).then_inc(pt_hi_done, 1)
                if more:
                    split_ctxT(b + 1)
                act.wait_ge(pc_made, b + 1)
                act.wait_ge(inv_set, b + 1)
                nc.scalar.activation(pc[:, :], bank(PCB, C, N), ACT.Copy,
                                     scale=row_inv[:, :]).then_inc(pc_scaled, 1)
                act.wait_ge(pcT_made, b + 1)
                nc.scalar.activation(q_hi[:, :, bass.ds(b * N, N)],
                                     bank(PTB5, KC * N).rearrange("p (c n) -> p c n", n=N),
                                     ACT.Copy).then_inc(at_hi_done, 1)
                act.wait_ge(w_used, J_GX + 1 + b)
                nc.scalar.activation(acc[:, bass.ds(b, 1), 0:H].rearrange("p k r -> p (k r)"), bank(GXB, H),
                                     ACT.Copy).then_inc(gx_saved, 1)
                if more:
                    split_ctx(b + 1)

            with act.Fori(0, B // 2 - 1) as i:
                b = 2 * i
                step(b, 0, True)
                step(b + 1, 1, True)
            step(B - 2, 0, True)
            step(B - 1, 1, False)
            split_w(J_MC + 1, 1)

            def mc_tile(k, u):
                act.wait_ge(mc_made, k + 1)
                src = ps[:, 2 * u * BANK:(2 * u + 2) * BANK].rearrange("p (h m) -> p h m", h=2)[:, :, 0:H]
                nc.scalar.activation(act_hi[:, bass.ds(k, 1), :].rearrange("p k (h r) -> p (k h) r", h=2), src,
                                     ACT.Copy)
                nc.scalar.activation(mc[:, bass.ds(k, 1), :].rearrange("p k (h r) -> p (k h) r", h=2), src,
                                     ACT.Copy).then_inc(mc_saved, 1)

            def mc_pair(q, slot):
                mc_tile(2 * q, 0)
                mc_tile(2 * q + 1, 1)
                split_w(J_MC + 2 + q, slot, (mc_made, 2 * q + 2))

            with act.Fori(0, KD // 4) as i:
                q = 2 * i
                mc_pair(q, 0)
                mc_pair(q + 1, 1)

            act.wait_ge(eps_set, 1)
            act.wait_ge(const_in, 32)

            def gate_step(t, k, h, slot, more):
                act.wait_ge(gate_summed, t + 1)
                nc.scalar.activation(gate[:, slot, :], gate[:, slot, :], ACT.Sigmoid,
                                     bias=bias_t[:, bass.ds(k, 1)]).then_inc(gate_done, 1)
                if more:
                    split_w(J_G2 + 2 + t, slot, (gate_made, t + 1))
                act.wait_ge(fused, t + 1)
                if not isinstance(t, int) or t >= 2:
                    act.wait_ge(summed, t - 1)
                rows = acc[:, bass.ds(k, 1), h * H:(h + 1) * H].rearrange("p k r -> p (k r)")
                nc.scalar.activation(square[:, slot, :], rows, ACT.Square).then_inc(squared, 1)
                act.wait_ge(squared, t + 1)
                nc.scalar.activation(rows, rows, ACT.Copy, scale=norm_t[:, bass.ds(k, 1)]).then_inc(weighted, 1)

            def root(h):
                act.wait_ge(mean_made, h + 1)
                nc.scalar.activation(rms_inv[:, h, :], bank(MSB, H), ACT.Sqrt,
                                     bias=eps_t[:, :]).then_inc(root_done, 1)

            gate_step(0, 0, 0, 0, True)
            gate_step(1, 1, 0, 1, True)
            with act.Fori(1, KD // 2) as i:
                t = 2 * i
                gate_step(t, t, 0, 0, True)
                gate_step(t + 1, t + 1, 0, 1, True)
            gate_step(KD, 0, 1, 0, True)
            gate_step(KD + 1, 1, 1, 1, True)
            root(0)
            with act.Fori(KD // 2 + 1, STEPS // 2 - 1) as i:
                t = 2 * i
                gate_step(t, t - KD, 1, 0, True)
                gate_step(t + 1, t + 1 - KD, 1, 1, True)
            gate_step(STEPS - 2, KD - 2, 1, 0, False)
            gate_step(STEPS - 1, KD - 1, 1, 1, False)
            root(1)

        @block.vector
        def _(dve):
            def minus(out, whole, hi):
                return nc.vector.tensor_tensor(out, whole, hi.bitcast(F32), ALU.subtract)

            def split_w(j, slot):
                dve.wait_ge(w_hi_done, j + 1)
                minus(w_lo[slot][:, :], w_stage[:, slot, :], w_hi[slot][:, :]).then_inc(w_lo_done, 1)

            def split_x(k):
                dve.wait_ge(x_hi_done, k + 1)
                minus(act_lo[:, k, :], acc[:, k, :], act_hi[:, k, :]).then_inc(x_lo_done, 1)

            def split_ctxT(b):
                for s in range(2):
                    dve.wait_ge(ct_hi_done, 2 * b + s + 1)
                    minus(ct_lo[:, 2 * s:2 * s + 2, :], ct_stage[:, 2 * s:2 * s + 2, :],
                          ct_hi[:, 2 * s:2 * s + 2, :]).then_inc(ct_lo_done, 1)

            nc.vector.memset(eps_t[:, :], EPS).then_inc(eps_set, 1)

            def split_ctx(b):
                dve.wait_ge(cn_hi_done, 2 * b + 1)
                minus(cn_lo[:, 0:3, :], cn_stage[:, 0:3, :], cn_hi[:, 0:3, :]).then_inc(cn_lo_done, 1)
                dve.wait_ge(cn_hi_done, 2 * b + 2)
                minus(cn_lo[:, 3:MT, :], cn_stage[:, 3:MT, :], cn_hi[:, 3:MT, :])
                minus(cn_lo[0:ML, MT, :], cn_stage[0:ML, MT, :], cn_hi[0:ML, MT, :]).then_inc(cn_lo_done, 1)

            split_x(0)
            split_w(0, 0)
            split_x(1)
            split_x(2)
            split_w(1, 1)
            split_x(3)
            split_x(4)
            split_w(2, 0)
            split_x(5)
            split_x(6)
            split_x(7)
            split_w(3, 1)
            split_ctxT(0)
            split_ctx(0)
            split_w(J_GX, 0)
            for h in range(2):
                for c in range(KC):
                    dve.wait_ge(q_hi_done, h * KC + c + 1)
                    done = minus(q_lo[:, c, h * H:(h + 1) * H], bank(c + 4 * h, H),
                                 q_hi[:, c, h * H:(h + 1) * H]).then_inc(q_lo_done, 1)

            def step(b, slot, more):
                dve.wait_ge(scores_made, b + 1)
                nc.vector.reduce_max(top_score[:, :], scores, AX.XY).then_inc(top_found, 1)
                dve.wait_ge(top_found, b + 1)
                nc.vector.tensor_scalar(neg_top[:, :], top_score[:, :], -float(D) ** -0.5, None,
                                        ALU.mult).then_inc(neg_top_set, 1)
                split_w(J_GX + 1 + b, 1 - slot)
                dve.wait_ge(exp_done, b + 1)
                nc.vector.reciprocal(row_inv[:, :], row_sum[:, :]).then_inc(inv_set, 1)
                dve.wait_ge(pt_hi_done, b + 1)
                minus(pt_lo[:, 0:MT, :], bank(PTB, MT * N).rearrange("p (t n) -> p t n", n=N), pt_hi[:, 0:MT, :])
                minus(pt_lo[0:ML, MT, :], bank(PTB5, N, ML, KC * N), pt_hi[0:ML, MT, :]).then_inc(pt_lo_done, 1)
                if more:
                    split_ctxT(b + 1)
                dve.wait_ge(at_hi_done, b + 1)
                minus(q_lo[:, :, bass.ds(b * N, N)], bank(PTB5, KC * N).rearrange("p (c n) -> p c n", n=N),
                      q_hi[:, :, bass.ds(b * N, N)]).then_inc(at_lo_done, 1)
                dve.wait_ge(w_used, J_GX + 1 + b)
                nc.vector.tensor_copy(acc[:, bass.ds(b, 1), H:R].rearrange("p k r -> p (k r)"),
                                      bank(GXB + 1, H)).then_inc(gx_saved, 1)
                if more:
                    split_ctx(b + 1)

            with dve.Fori(0, B // 2 - 1) as i:
                b = 2 * i
                step(b, 0, True)
                step(b + 1, 1, True)
            step(B - 2, 0, True)
            step(B - 1, 1, False)
            split_w(J_MC + 1, 1)

            dve.wait_ge(mc_made, 1)
            nc.vector.memset(mean_w[:, :], 1.0 / D).then_inc(mean_w_set, 1)
            nc.vector.memset(square_sum[:, :, :], 0.0).then_inc(mean_w_set, 1)

            def mc_tile(k, u):
                dve.wait_ge(mc_saved, k + 1)
                minus(*(a[:, bass.ds(k, 1), :].rearrange("p k r -> p (k r)") for a in (act_lo, mc, act_hi)))\
                    .then_inc(mc_lo_done, 1)

            def mc_pair(q, slot):
                mc_tile(2 * q, 0)
                mc_tile(2 * q + 1, 1)
                split_w(J_MC + 2 + q, slot)

            with dve.Fori(0, KD // 4) as i:
                q = 2 * i
                mc_pair(q, 0)
                mc_pair(q + 1, 1)
            dve.wait_ge(mean_w_set, 2)
            dve.wait_ge(xa_in, 16)

            def gate_step(t, k, h, slot, more):
                rows = acc[:, bass.ds(k, 1), h * H:(h + 1) * H].rearrange("p k r -> p (k r)")
                mc_rows = mc[:, bass.ds(k, 1), h * H:(h + 1) * H].rearrange("p k r -> p (k r)")
                xa_rows = x_again[:, bass.ds(k, 1), h * H:(h + 1) * H].rearrange("p k r -> p (k r)")
                dve.wait_ge(gate_made, t + 1)
                nc.vector.tensor_tensor(gate[:, slot, :], bank(G2B + slot, H), rows, ALU.add).then_inc(gate_summed, 1)
                dve.wait_ge(gate_done, t + 1)
                nc.vector.tensor_tensor(gate[:, slot, :], gate[:, slot, :], mc_rows, ALU.mult).then_inc(gated, 1)
                dve.wait_ge(gated, t + 1)
                nc.vector.tensor_tensor(rows, gate[:, slot, :], xa_rows, ALU.add).then_inc(fused, 1)
                if more:
                    split_w(J_G2 + 2 + t, slot)
                dve.wait_ge(squared, t + 1)
                if not isinstance(t, int) or t > 0:
                    dve.wait_ge(summed, t)
                nc.vector.tensor_tensor(square_sum[:, h, :], square_sum[:, h, :], square[:, slot, :],
                                        ALU.add).then_inc(summed, 1)

            def invert(h):
                dve.wait_ge(root_done, h + 1)
                nc.vector.reciprocal(rms_inv[:, h, :], rms_inv[:, h, :]).then_inc(inv_done, 1)

            gate_step(0, 0, 0, 0, True)
            gate_step(1, 1, 0, 1, True)
            with dve.Fori(1, KD // 2) as i:
                t = 2 * i
                gate_step(t, t, 0, 0, True)
                gate_step(t + 1, t + 1, 0, 1, True)
            gate_step(KD, 0, 1, 0, True)
            gate_step(KD + 1, 1, 1, 1, True)
            invert(0)
            with dve.Fori(KD // 2 + 1, STEPS // 2 - 1) as i:
                t = 2 * i
                gate_step(t, t - KD, 1, 0, True)
                gate_step(t + 1, t + 1 - KD, 1, 1, True)
            gate_step(STEPS - 2, KD - 2, 1, 0, False)
            gate_step(STEPS - 1, KD - 1, 1, 1, False)
            invert(1)
            dve.wait_ge(weighted, STEPS)
            dve.wait_ge(inv_done, 2)
            for k in range(KD):
                nc.vector.tensor_tensor(acc[:, k, H:R], acc[:, k, H:R], rms_inv[:, 1, :],
                                        ALU.mult).then_inc(out1_done, 1)

        @block.gpsimd
        def _(pool):
            nc.gpsimd.memset(ident[:, :], 0.0).then_inc(ident_zeroed, 1)
            pool.wait_ge(ident_zeroed, 1)
            nc.gpsimd.affine_select(out=ident[:, :], in_=ident[:, :], compare_op=ALU.not_equal, fill=1.0,
                                    base=0, pattern=[[-1, N]], channel_multiplier=1).then_inc(consts_set, 1)

            def copy_q(b):
                nc.gpsimd.tensor_copy(qb_hi[:, :, :], q_hi[:, :, bass.ds(b * N, N)])
                nc.gpsimd.tensor_copy(qb_lo[:, :, :], q_lo[:, :, bass.ds(b * N, N)]).then_inc(qb_copied, 1)

            pool.wait_ge(q_lo_done, KC)
            copy_q(0)
            with pool.Fori(1, B) as b:
                pool.wait_ge(scores_made, b)
                copy_q(b)

            pool.wait_ge(inv_done, 1)
            pool.wait_ge(weighted, KD)
            for k in range(KD):
                nc.gpsimd.tensor_tensor(acc[:, k, 0:H], acc[:, k, 0:H], rms_inv[:, 0, :],
                                        ALU.mult).then_inc(out0_done, 1)


def kernel(x, ctx_1024, L0_xattn_W_mem, L0_xattn_W_gate, L0_xattn_b_gate, L0_xattn_norm_w):
    import numpy as np
    import concourse.bacc as bacc
    from concourse.bass_utils import run_bass_kernel_spmd

    x, ctx, wm, wg = (np.asarray(a) for a in (x, ctx_1024, L0_xattn_W_mem, L0_xattn_W_gate))
    wg = wg.reshape(KD, P, 2, KD, P).transpose(2, 0, 4, 3, 1)
    arrays = {
        "xT": x.reshape(R, D).T,
        "ctxT": ctx.transpose(0, 2, 1),
        "ctxN": ctx,
        "w_mem": wm.reshape(KD // 2, 2, P, C).transpose(0, 2, 1, 3).reshape(KD // 2, P, WB),
        "w_gate_x": wg[0].reshape(KD, P, WB),
        "w_mem_t": wm.reshape(KD // 2, 2, P, KC, P).transpose(0, 4, 1, 3, 2).reshape(KD // 2, P, WB),
        "w_gate_mc": wg[1].reshape(KD, P, WB),
        "b_gate": np.asarray(L0_xattn_b_gate).reshape(KD, P).T,
        "norm_w": np.asarray(L0_xattn_norm_w).reshape(KD, P).T,
    }
    arrays = {k: np.ascontiguousarray(v) for k, v in arrays.items()}
    nc = bacc.Bacc("TRN2", target_bir_lowering=False, num_devices=1)
    args = [nc.dram_tensor(k, v.shape, mybir.dt.from_np(v.dtype), kind="ExternalInput").ap()
            for k, v in arrays.items()]
    out = nc.dram_tensor("outT", (D, R), mybir.dt.float32, kind="ExternalOutput").ap()
    build(nc, *args, out)
    got = run_bass_kernel_spmd(nc, [arrays], core_ids=[0]).results[0]["outT"]
    return np.ascontiguousarray(got.T).reshape(B, N, D)
```

```python
from contextlib import ExitStack

import concourse.bass as bass
from concourse import mybir

B, N, D = 8, 100, 1024
M, C = 722, 512
P = 128
R = B * N
H = R // 2
KD, KC = D // P, C // P
MT = M // P
ML = M - MT * P
MH = M // 2
BANK = 512
WB = KD * P
EPS = 1e-6
NH = H // N
GROUPS = ((0, NH), (NH, NH // 2), (NH + NH // 2, NH // 2))

J_MEM = 0
J_GX = J_MEM + KD // 2
J_MC = J_GX + KD
J_G2 = J_MC + KD // 2
STEPS = 2 * KD
PARTS = STEPS + 1


def build(nc, xT, ctxT, ctxN, w_mem, w_gate_x, w_mem_t, w_gate_mc, b_gate, norm_w, outT):
    F32, F32R = mybir.dt.float32, mybir.dt.float32r
    ALU, ACT, AX = mybir.AluOpType, mybir.ActivationFunctionType, mybir.AxisListType

    top = ExitStack()
    with top:
        def sb(scope, name, shape, dt=F32):
            return scope.enter_context(nc.sbuf_tensor(name, shape, dt))

        def sem(name):
            return top.enter_context(nc.semaphore(name))

        act_hi = sb(top, "act_hi", [P, KD, R], F32R)
        act_lo = sb(top, "act_lo", [P, KD, R], F32R)
        q_hi = sb(top, "q_hi", [P, KC, R], F32R)
        q_lo = sb(top, "q_lo", [P, KC, R], F32R)
        acc = sb(top, "acc", [P, KD, R])
        w_stage = sb(top, "w_stage", [P, 2, WB])
        w_hi = [sb(top, f"w_hi{i}", [P, WB], F32R) for i in range(2)]
        w_lo = [sb(top, f"w_lo{i}", [P, WB], F32R) for i in range(2)]
        ident = sb(top, "ident", [N, N])
        bias_t = sb(top, "bias_t", [P, KD])
        norm_t = sb(top, "norm_t", [P, KD])
        top_score = sb(top, "top_score", [N, 2])
        neg_top = sb(top, "neg_top", [N, 1])
        row_sum = sb(top, "row_sum", [N, 1])
        row_inv = sb(top, "row_inv", [N, 1])

        with ExitStack() as attn:
            ct_stage = sb(attn, "ct_stage", [P, KC, M])
            cn_stage = sb(attn, "cn_stage", [P, MT + 1, C])
            ct_hi = sb(attn, "ct_hi", [P, KC, M], F32R)
            ct_lo = sb(attn, "ct_lo", [P, KC, M], F32R)
            cn_hi = sb(attn, "cn_hi", [P, MT + 1, C], F32R)
            cn_lo = sb(attn, "cn_lo", [P, MT + 1, C], F32R)
            qb_hi = sb(attn, "qb_hi", [P, KC, N], F32R)
            qb_lo = sb(attn, "qb_lo", [P, KC, N], F32R)
            probs = sb(attn, "probs", [N, M])
            pt_hi = sb(attn, "pt_hi", [P, MT + 1, N], F32R)
            pt_lo = sb(attn, "pt_lo", [P, MT + 1, N], F32R)
            pc = sb(attn, "pc", [N, C])
        mc = sb(top, "mc", [P, KD, R])
        x_again = sb(top, "x_again", [P, KD, R])
        gate = sb(top, "gate", [P, 2, H])
        square = sb(top, "square", [P, 2, H])
        square_sum = sb(top, "square_sum", [P, 2, H])
        mean_w = sb(top, "mean_w", [P, 1])
        ones = sb(top, "ones", [N, P])
        minus_half = sb(top, "minus_half", [N, B])
        rms = sb(top, "rms", [N, B])
        rms_diag = sb(top, "rms_diag", [N, B, N])

        ps = top.enter_context(nc.psum_tensor("ps", [P, 8 * BANK], F32))

        def bank(i, cols, rows=P, at=0):
            return ps[0:rows, i * BANK + at:i * BANK + at + cols]

        scores = ps[0:N, 0:2 * (BANK + 1)].rearrange("p (h m) -> p h m", h=2)[:, :, 0:MH]
        GXB, PTB, PTB5, PCB = 2, 4, 5, 6
        G2B, MSB, RIB = 4, (6, 2, 1), (7, 3, 0)
        gx_ps = ps[:, GXB * BANK:(GXB + 2) * BANK].rearrange("p (h m) -> p h m", h=2)[:, :, 0:H]

        x_in = [sem(f"x_in{k}") for k in range(KD)]
        w_first_in, x_first_in = sem("w_first_in"), sem("x_first_in")
        w_in = [sem(f"w_in{s}") for s in range(2)]
        ct_in = [sem(f"ct_in{s}") for s in range(2)]
        cn_in = [sem(f"cn_in{s}") for s in range(2)]
        const_in = sem("const_in")
        xa_in = sem("xa_in")
        stored = sem("stored")
        x_hi_done, x_lo_done = sem("x_hi_done"), sem("x_lo_done")
        w_hi_done, w_lo_done = sem("w_hi_done"), sem("w_lo_done")
        first_hi_done, first_lo_done = sem("first_hi_done"), sem("first_lo_done")
        ct_hi_done, ct_lo_done = sem("ct_hi_done"), sem("ct_lo_done")
        cn_hi_done, cn_lo_done = sem("cn_hi_done"), sem("cn_lo_done")
        q_hi_done, q_lo_done = sem("q_hi_done"), sem("q_lo_done")
        pt_hi_done, pt_lo_done = sem("pt_hi_done"), sem("pt_lo_done")
        at_hi_done, at_lo_done = sem("at_hi_done"), sem("at_lo_done")
        mc_lo_done = sem("mc_lo_done")
        w_used = sem("w_used")
        q_made = sem("q_made")
        scores_made = sem("scores_made")
        probsT_made = sem("probsT_made")
        pc_made = sem("pc_made")
        pcT_made = sem("pcT_made")
        mc_made = sem("mc_made")
        gate_made = sem("gate_made")
        mean_made = sem("mean_made")
        consts_set = sem("consts_set")
        ident_zeroed = sem("ident_zeroed")
        qb_copied = sem("qb_copied")
        top_found, neg_top_set = sem("top_found"), sem("neg_top_set")
        exp_done = sem("exp_done")
        inv_set = sem("inv_set")
        pc_scaled = sem("pc_scaled")
        gx_saved = sem("gx_saved")
        mc_saved = sem("mc_saved")
        gate_summed = sem("gate_summed")
        gate_done = sem("gate_done")
        gated, fused = sem("gated"), sem("fused")
        squared = sem("squared")
        summed = sem("summed")
        mean_copied = sem("mean_copied")
        rooted = sem("rooted")
        diag_done = sem("diag_done")
        inv_made = sem("inv_made")
        mean_w_set = sem("mean_w_set")
        out_done = [sem(f"out_done{g}") for g in range(3)]

        ct_rows = ctxT.rearrange("b c m -> (b c) m")
        cn_rows = ctxN.rearrange("b m c -> (b m) c")
        wgx_rows = w_gate_x.rearrange("t p n -> (t p) n")
        wg2_rows = w_gate_mc.rearrange("t p n -> (t p) n")

        block = top.enter_context(nc.Block())

        @block.sync
        def _(sp):
            def load_x(k):
                sp.dma_start(acc[:, k, :], xT[k * P:(k + 1) * P, :]).then_inc(x_in[k], 16)

            def load_w(j, src, slot):
                if not isinstance(j, int) or j >= 2:
                    sp.wait_ge(w_lo_done, j - 1)
                sp.dma_start(w_stage[:, slot, :], src).then_inc(w_in[slot], 16)

            def load_ctxT(b, first=False):
                for s in range(2):
                    if not first:
                        sp.wait_ge(ct_lo_done, 2 * b - 1 + s)
                    sp.dma_start(ct_stage[:, 2 * s:2 * s + 2, :],
                                 ct_rows[bass.ds(b * C + s * 2 * P, 2 * P), :]
                                 .rearrange("(k p) m -> p k m", p=P)).then_inc(ct_in[s], 16)

            def load_ctx(b, first=False):
                if not first:
                    sp.wait_ge(cn_lo_done, 2 * b - 1)
                sp.dma_start(cn_stage[:, 0:3, :], cn_rows[bass.ds(b * M, 3 * P), :]
                             .rearrange("(t p) c -> p t c", p=P)).then_inc(cn_in[0], 16)
                if not first:
                    sp.wait_ge(cn_lo_done, 2 * b)
                sp.dma_start(cn_stage[:, 3:MT, :], cn_rows[bass.ds(b * M + 3 * P, (MT - 3) * P), :]
                             .rearrange("(t p) c -> p t c", p=P)).then_inc(cn_in[1], 16)
                sp.dma_start(cn_stage[0:ML, MT, :],
                             cn_rows[bass.ds(b * M + MT * P, ML), :]).then_inc(cn_in[1], 16)

            sp.dma_start(w_stage[:, 0, 0:C], w_mem[0][:, 0:C]).then_inc(w_first_in, 16)
            sp.dma_start(acc[:, 0, 0:H], xT[0:P, 0:H]).then_inc(x_first_in, 16)
            sp.dma_start(acc[:, 0, H:R], xT[0:P, H:R]).then_inc(x_in[0], 16)
            sp.dma_start(w_stage[:, 0, C:WB], w_mem[0][:, C:WB]).then_inc(w_in[0], 16)
            load_x(1)
            load_x(2)
            load_w(1, w_mem[1], 1)
            load_x(3)
            load_x(4)
            load_x(5)
            load_w(2, w_mem[2], 0)
            load_x(6)
            load_x(7)
            load_w(3, w_mem[3], 1)
            load_ctxT(0, first=True)
            load_ctx(0, first=True)
            sp.dma_start(bias_t[:, :], b_gate).then_inc(const_in, 16)
            sp.dma_start(norm_t[:, :], norm_w).then_inc(const_in, 16)
            load_w(J_GX, w_gate_x[0], 0)
            load_w(J_GX + 1, w_gate_x[1], 1)

            def ahead(b, slot):
                load_w(J_GX + 2 + b, wgx_rows[bass.ds((b + 2) * P, P), :], slot)
                load_ctxT(b + 1)
                load_ctx(b + 1)

            with sp.Fori(0, B // 2 - 1) as i:
                b = 2 * i
                ahead(b, 0)
                ahead(b + 1, 1)
            load_w(J_MC, w_mem_t[0], 0)
            load_ctxT(B - 1)
            load_ctx(B - 1)
            load_w(J_MC + 1, w_mem_t[1], 1)
            load_w(J_MC + 2, w_mem_t[2], 0)
            load_w(J_MC + 3, w_mem_t[3], 1)
            load_w(J_G2, w_gate_mc[0], 0)

            sp.wait_ge(mc_made, 1)
            sp.dma_start(x_again[:, :, :], xT.rearrange("(k p) r -> p k r", p=P)).then_inc(xa_in, 16)
            load_w(J_G2 + 1, w_gate_mc[1], 1)
            with sp.Fori(0, KD // 2 - 1) as i:
                for u in range(2):
                    load_w(J_G2 + 2 + 2 * i + u, wg2_rows[bass.ds((2 * i + u + 2) * P, P), :], u)
            with sp.Fori(0, KD // 2) as i:
                for u in range(2):
                    load_w(J_G2 + KD + 2 * i + u, wg2_rows[bass.ds((2 * i + u) * P, P), :], u)
            out_v = outT.rearrange("(k p) r -> p k r", p=P)
            for g, (b0, n) in enumerate(GROUPS):
                for k in range(0, KD, 2):
                    sp.wait_ge(out_done[g], k + 2)
                    sp.dma_start(out_v[:, k:k + 2, b0 * N:(b0 + n) * N],
                                 acc[:, k:k + 2, b0 * N:(b0 + n) * N]).then_inc(stored, 16)
            sp.wait_ge(stored, 16 * len(GROUPS) * KD // 2)

        @block.tensor
        def _(pe):
            def three(outs, weight, stream, first, last):
                (wh, wl), done = weight, None
                for wgt, part in ((wh, 0), (wh, 1), (wl, 0)):
                    for h, o in enumerate(outs):
                        done = nc.tensor.matmul(o, wgt, stream[h][part],
                                                start=first and wgt is wh and part == 0,
                                                stop=last and wgt is wl)
                return done

            def w_tile(slot, i):
                return w_hi[slot][:, i * P:(i + 1) * P], w_lo[slot][:, i * P:(i + 1) * P]

            def halves(hi, lo, k):
                return [(hi[:, k, h * H:(h + 1) * H], lo[:, k, h * H:(h + 1) * H]) for h in range(2)]

            for k in range(KD):
                last_k = k == KD - 1
                if k == 0:
                    for h in range(2):
                        pe.wait_ge(*((x_lo_done, 1) if h else (first_lo_done, 2)))
                        for c in range(KC):
                            three([bank(c + 4 * h, H)], w_tile(0, c), halves(act_hi, act_lo, 0)[h:h + 1],
                                  True, False)
                    continue
                if k == 1 or k % 2 == 0:
                    pe.wait_ge(w_lo_done, k // 2 + 1)
                pe.wait_ge(x_lo_done, k + 1)
                if not last_k:
                    for c in range(KC):
                        done = three([bank(c, H), bank(c + 4, H)], w_tile(k // 2 % 2, k % 2 * 4 + c),
                                     halves(act_hi, act_lo, k), False, False)
                else:
                    for h in range(2):
                        for c in range(KC):
                            done = three([bank(c + 4 * h, H)], w_tile(k // 2 % 2, k % 2 * 4 + c),
                                         halves(act_hi, act_lo, k)[h:h + 1], False, True)
                            if (h, c) != (1, KC - 1):
                                done.then_inc(q_made, 1)
                if k % 2 == 1:
                    done.then_inc(w_used, 1)

            def gate_x(slot, k0, k1):
                for k in range(k0, k1):
                    last = three([bank(GXB, H), bank(GXB + 1, H)], w_tile(slot, k),
                                 halves(act_hi, act_lo, k), k == 0, k == KD - 1)
                return last

            def step(b, slot, cuts):
                def fill(i):
                    if cuts[i] < cuts[i + 1]:
                        last = gate_x(slot, cuts[i], cuts[i + 1])
                        if cuts[i + 1] == KD:
                            last.then_inc(w_used, 1)

                if cuts[1] > 0:
                    pe.wait_ge(w_lo_done, J_GX + 1 + b)
                    fill(0)
                pe.wait_ge(ct_lo_done, 2 * b + 2)
                pe.wait_ge(qb_copied, 2 * b + 2)
                for h in range(2):
                    at = h * (MH - 1)
                    for k in range(KC):
                        for lhs, rhs, part in ((qb_hi, ct_hi, 0), (qb_hi, ct_lo, 1), (qb_lo, ct_hi, 2)):
                            done = nc.tensor.matmul(bank(h, MH + 1, N), lhs[:, k, :],
                                                    rhs[:, k, at:at + MH + 1],
                                                    start=k == 0 and part == 0,
                                                    stop=k == KC - 1 and part == 2)
                    done.then_inc(scores_made, 1)
                if cuts[1] == 0:
                    pe.wait_ge(w_lo_done, J_GX + 1 + b)
                    pe.wait_ge(gx_saved, 2 * b)
                fill(1)
                pe.wait_ge(exp_done, b + 1)
                for t in range(MT + 1):
                    rows = P if t < MT else ML
                    o = bank(PTB, N, P, t * N) if t < MT else bank(PTB5, N, ML, KC * N)
                    done = nc.tensor.transpose(o, probs[:, t * P:t * P + rows], ident[:, :])
                done.then_inc(probsT_made, 1)
                fill(2)
                pe.wait_ge(pt_lo_done, b + 1)
                pe.wait_ge(cn_lo_done, 2 * b + 2)
                for t in range(MT + 1):
                    rows = P if t < MT else ML
                    for lhs, rhs, part in ((pt_hi, cn_hi, 0), (pt_hi, cn_lo, 1), (pt_lo, cn_hi, 2)):
                        done = nc.tensor.matmul(bank(PCB, C, N), lhs[0:rows, t, :], rhs[0:rows, t, :],
                                                start=t == 0 and part == 0, stop=t == MT and part == 2)
                done.then_inc(pc_made, 1)
                fill(3)
                pe.wait_ge(pc_scaled, b + 1)
                for c in range(KC):
                    done = nc.tensor.transpose(bank(PTB5, N, P, c * N), pc[:, c * P:(c + 1) * P],
                                               ident[:, :])
                done.then_inc(pcT_made, 1)

            pe.wait_ge(consts_set, 1)
            pe.wait_ge(q_lo_done, KC)
            step(0, 0, (0, 3, 5, 7, KD))
            CUTS = (0, 0, 4, 7, KD)
            step(1, 1, CUTS)
            with pe.Fori(1, B // 2) as i:
                step(2 * i, 0, CUTS)
                step(2 * i + 1, 1, CUTS)

            pe.wait_ge(at_lo_done, B)
            pe.wait_ge(gx_saved, 2 * B)

            def mc_block(q, slot, free):
                pe.wait_ge(w_lo_done, J_MC + 1 + q)
                for u in range(2):
                    if free:
                        pe.wait_ge(mc_saved, 2 * q + u - 1)
                    for k in range(KC):
                        done = three([bank(2 * u, H), bank(2 * u + 1, H)], w_tile(slot, u * KC + k),
                                     halves(q_hi, q_lo, k), k == 0, k == KC - 1)
                    done.then_inc(mc_made, 1)

            mc_block(0, 0, False)
            mc_block(1, 1, True)
            mc_block(2, 0, True)
            mc_block(3, 1, True)

            def gate_mc(t, h, slot, first=False, part=slice(0, H), psum=None):
                if part.start == 0:
                    pe.wait_ge(w_lo_done, J_G2 + 1 + t)
                if not first:
                    pe.wait_ge(gate_summed, t - 1 + (part.start > 0))
                for k in range(KD):
                    if first and slot == 0:
                        pe.wait_ge(mc_lo_done, k + 1)
                    stream = [(act_hi[:, k, h * H + part.start:h * H + part.stop],
                               act_lo[:, k, h * H + part.start:h * H + part.stop])]
                    o = bank(G2B + (slot if psum is None else psum), part.stop - part.start, P, part.start)
                    done = three([o], w_tile(slot, k), stream, k == 0, k == KD - 1)
                done.then_inc(gate_made, 1)

            def mean_square(g, late=None):
                b0, n = GROUPS[g]
                for i in range(n):
                    at = (b0 + i) % NH * N
                    o = bank(MSB[g], 1, N, i)
                    done = nc.tensor.matmul(o, square_sum[:, b0 // NH, at:at + N], mean_w[:, :],
                                            start=True, stop=late is None)
                    if late is not None:
                        done = nc.tensor.matmul(o, square[:, late, at:at + N], mean_w[:, :],
                                                start=False, stop=True)
                done.then_inc(mean_made, 1)

            def inverse(g):
                b0, n = GROUPS[g]
                pe.wait_ge(diag_done, b0 + n)
                for i in range(n):
                    done = nc.tensor.matmul(bank(RIB[g], N, P, i * N), ones[:, :], rms_diag[:, b0 + i, :],
                                            start=True, stop=True)
                done.then_inc(inv_made, 1)

            gate_mc(0, 0, 0, first=True)
            gate_mc(1, 0, 1, first=True)
            with pe.Fori(1, KD // 2) as i:
                gate_mc(2 * i, 0, 0)
                gate_mc(2 * i + 1, 0, 1)
            gate_mc(KD, 1, 0)
            pe.wait_ge(summed, KD)
            mean_square(0)
            gate_mc(KD + 1, 1, 1)
            inverse(0)
            with pe.Fori(KD // 2 + 1, STEPS // 2 - 1) as i:
                gate_mc(2 * i, 1, 0)
                gate_mc(2 * i + 1, 1, 1)
            gate_mc(STEPS - 2, 1, 0)
            gate_mc(STEPS - 1, 1, 1, part=slice(0, H // 2))
            gate_mc(STEPS - 1, 1, 1, part=slice(H // 2, H), psum=0)
            pe.wait_ge(summed, STEPS - 1)
            pe.wait_ge(squared, STEPS)
            mean_square(1, late=1)
            inverse(1)
            pe.wait_ge(squared, STEPS + 1)
            mean_square(2, late=0)
            inverse(2)

        @block.scalar
        def _(act):
            def split_w(j, slot, free=None):
                act.wait_ge(w_in[slot], 8 * (j - slot) + 16)
                if free is not None:
                    act.wait_ge(*free)
                elif not isinstance(j, int) or j >= 2:
                    act.wait_ge(w_used, j - 1)
                nc.scalar.activation(w_hi[slot][:, :], w_stage[:, slot, :], ACT.Copy).then_inc(w_hi_done, 1)

            def split_x(k):
                act.wait_ge(x_in[k], 16)
                nc.scalar.activation(act_hi[:, k, :], acc[:, k, :], ACT.Copy).then_inc(x_hi_done, 1)

            def split_ctxT(b):
                if not isinstance(b, int) or b > 0:
                    act.wait_ge(scores_made, 2 * b)
                for s in range(2):
                    act.wait_ge(ct_in[s], 16 * b + 16)
                    nc.scalar.activation(ct_hi[:, 2 * s:2 * s + 2, :], ct_stage[:, 2 * s:2 * s + 2, :],
                                         ACT.Copy).then_inc(ct_hi_done, 1)

            def split_ctx(b, part):
                if part == 0:
                    if not isinstance(b, int) or b > 0:
                        act.wait_ge(pc_made, b)
                    act.wait_ge(cn_in[0], 16 * b + 16)
                    nc.scalar.activation(cn_hi[:, 0:3, :], cn_stage[:, 0:3, :], ACT.Copy).then_inc(cn_hi_done, 1)
                else:
                    act.wait_ge(cn_in[1], 32 * b + 32)
                    nc.scalar.activation(cn_hi[:, 3:MT, :], cn_stage[:, 3:MT, :], ACT.Copy)
                    nc.scalar.activation(cn_hi[0:ML, MT, :], cn_stage[0:ML, MT, :],
                                         ACT.Copy).then_inc(cn_hi_done, 1)

            act.wait_ge(w_first_in, 16)
            nc.scalar.activation(w_hi[0][:, 0:C], w_stage[:, 0, 0:C], ACT.Copy).then_inc(first_hi_done, 1)
            act.wait_ge(x_first_in, 16)
            nc.scalar.activation(act_hi[:, 0, 0:H], acc[:, 0, 0:H], ACT.Copy).then_inc(first_hi_done, 1)
            act.wait_ge(x_in[0], 16)
            nc.scalar.activation(act_hi[:, 0, H:R], acc[:, 0, H:R], ACT.Copy).then_inc(x_hi_done, 1)
            act.wait_ge(w_in[0], 16)
            nc.scalar.activation(w_hi[0][:, C:WB], w_stage[:, 0, C:WB], ACT.Copy).then_inc(w_hi_done, 1)
            split_x(1)
            split_x(2)
            split_w(1, 1)
            split_x(3)
            split_x(4)
            split_w(2, 0)
            split_x(5)
            split_x(6)
            split_x(7)
            split_w(3, 1)
            split_ctxT(0)
            split_ctx(0, 0)
            split_ctx(0, 1)
            split_w(J_GX, 0)

            def copy_q(b):
                nc.scalar.activation(qb_hi[:, :, :], q_hi[:, :, bass.ds(b * N, N)].bitcast(F32),
                                     ACT.Copy).then_inc(qb_copied, 1)

            for h in range(2):
                for c in range(KC):
                    if (h, c) != (1, KC - 1):
                        act.wait_ge(q_made, h * KC + c + 1)
                    else:
                        act.wait_ge(w_used, KD // 2)
                    nc.scalar.activation(q_hi[:, c, h * H:(h + 1) * H], bank(c + 4 * h, H),
                                         ACT.Copy).then_inc(q_hi_done, 1)
                if h == 0:
                    act.wait_ge(q_hi_done, KC)
                    copy_q(0)
            act.wait_ge(q_hi_done, 2 * KC)

            def step(b, slot, more):
                act.wait_ge(neg_top_set, b + 1)
                nc.scalar.activation(probs[:, :].rearrange("p (h m) -> p h m", h=2), scores, ACT.Exp,
                                     bias=neg_top[:, :], scale=float(D) ** -0.5,
                                     accum_out=row_sum[:, :]).then_inc(exp_done, 1)
                split_w(J_GX + 1 + b, 1 - slot)
                if not isinstance(b, int) or b > 0:
                    split_ctx(b, 1)
                if more:
                    copy_q(b + 1)
                act.wait_ge(probsT_made, b + 1)
                nc.scalar.activation(pt_hi[:, 0:MT, :], bank(PTB, MT * N).rearrange("p (t n) -> p t n", n=N),
                                     ACT.Copy)
                nc.scalar.activation(pt_hi[0:ML, MT, :], bank(PTB5, N, ML, KC * N), ACT.Copy).then_inc(pt_hi_done, 1)
                if more:
                    split_ctxT(b + 1)
                act.wait_ge(pc_made, b + 1)
                act.wait_ge(inv_set, b + 1)
                nc.scalar.activation(pc[:, :], bank(PCB, C, N), ACT.Copy,
                                     scale=row_inv[:, :]).then_inc(pc_scaled, 1)
                act.wait_ge(pcT_made, b + 1)
                nc.scalar.activation(acc[:, bass.ds(b, 1), 0:H].rearrange("p k r -> p (k r)"), bank(GXB, H),
                                     ACT.Copy).then_inc(gx_saved, 1)
                nc.scalar.activation(q_hi[:, :, bass.ds(b * N, N)],
                                     bank(PTB5, KC * N).rearrange("p (c n) -> p c n", n=N),
                                     ACT.Copy).then_inc(at_hi_done, 1)
                if more:
                    split_ctx(b + 1, 0)

            step(0, 0, True)
            step(1, 1, True)
            with act.Fori(1, B // 2 - 1) as i:
                step(2 * i, 0, True)
                step(2 * i + 1, 1, True)
            step(B - 2, 0, True)
            step(B - 1, 1, False)
            split_w(J_MC + 1, 1)

            def mc_tile(k, u):
                act.wait_ge(mc_made, k + 1)
                src = ps[:, 2 * u * BANK:(2 * u + 2) * BANK].rearrange("p (h m) -> p h m", h=2)[:, :, 0:H]
                nc.scalar.activation(act_hi[:, bass.ds(k, 1), :].rearrange("p k (h r) -> p (k h) r", h=2), src,
                                     ACT.Copy)
                nc.scalar.activation(mc[:, bass.ds(k, 1), :].rearrange("p k (h r) -> p (k h) r", h=2), src,
                                     ACT.Copy).then_inc(mc_saved, 1)

            def mc_pair(q, slot):
                mc_tile(2 * q, 0)
                mc_tile(2 * q + 1, 1)
                split_w(J_MC + 2 + q, slot, (mc_made, 2 * q + 2))

            with act.Fori(0, KD // 4) as i:
                q = 2 * i
                mc_pair(q, 0)
                mc_pair(q + 1, 1)

            act.wait_ge(const_in, 32)

            def gate_step(t, k, h, slot, more, part=slice(0, H)):
                act.wait_ge(gate_summed, t + 1)
                nc.scalar.activation(gate[:, slot, part], gate[:, slot, part], ACT.Sigmoid,
                                     bias=bias_t[:, bass.ds(k, 1)]).then_inc(gate_done, 1)
                if more:
                    split_w(J_G2 + 2 + t, slot, (gate_made, t + 1))
                act.wait_ge(fused, t + 1)
                if not isinstance(t, int) or t >= 2:
                    act.wait_ge(summed, t - 1)
                rows = acc[:, bass.ds(k, 1), h * H + part.start:h * H + part.stop].rearrange("p k r -> p (k r)")
                nc.scalar.activation(square[:, slot, part], rows, ACT.Square).then_inc(squared, 1)

            gate_step(0, 0, 0, 0, True)
            gate_step(1, 1, 0, 1, True)
            with act.Fori(1, KD // 2) as i:
                gate_step(2 * i, 2 * i, 0, 0, True)
                gate_step(2 * i + 1, 2 * i + 1, 0, 1, True)
            with act.Fori(KD // 2, STEPS // 2 - 1) as i:
                gate_step(2 * i, 2 * i - KD, 1, 0, True)
                gate_step(2 * i + 1, 2 * i + 1 - KD, 1, 1, True)
            gate_step(STEPS - 2, KD - 2, 1, 0, False)
            gate_step(STEPS - 1, KD - 1, 1, 1, False, slice(0, H // 2))
            gate_step(STEPS, KD - 1, 1, 0, False, slice(H // 2, H))

        @block.vector
        def _(dve):
            def minus(out, whole, hi):
                return nc.vector.tensor_tensor(out, whole, hi.bitcast(F32), ALU.subtract)

            def split_w(j, slot):
                dve.wait_ge(w_hi_done, j + 1)
                minus(w_lo[slot][:, :], w_stage[:, slot, :], w_hi[slot][:, :]).then_inc(w_lo_done, 1)

            def split_x(k):
                dve.wait_ge(x_hi_done, k + 1)
                minus(act_lo[:, k, :], acc[:, k, :], act_hi[:, k, :]).then_inc(x_lo_done, 1)

            def split_ctxT(b):
                for s in range(2):
                    dve.wait_ge(ct_hi_done, 2 * b + s + 1)
                    minus(ct_lo[:, 2 * s:2 * s + 2, :], ct_stage[:, 2 * s:2 * s + 2, :],
                          ct_hi[:, 2 * s:2 * s + 2, :]).then_inc(ct_lo_done, 1)

            def split_ctx(b, part):
                dve.wait_ge(cn_hi_done, 2 * b + part + 1)
                if part == 0:
                    minus(cn_lo[:, 0:3, :], cn_stage[:, 0:3, :], cn_hi[:, 0:3, :]).then_inc(cn_lo_done, 1)
                else:
                    minus(cn_lo[:, 3:MT, :], cn_stage[:, 3:MT, :], cn_hi[:, 3:MT, :])
                    minus(cn_lo[0:ML, MT, :], cn_stage[0:ML, MT, :], cn_hi[0:ML, MT, :]).then_inc(cn_lo_done, 1)

            dve.wait_ge(first_hi_done, 1)
            minus(w_lo[0][:, 0:C], w_stage[:, 0, 0:C], w_hi[0][:, 0:C]).then_inc(first_lo_done, 1)
            dve.wait_ge(first_hi_done, 2)
            minus(act_lo[:, 0, 0:H], acc[:, 0, 0:H], act_hi[:, 0, 0:H]).then_inc(first_lo_done, 1)
            dve.wait_ge(x_hi_done, 1)
            minus(act_lo[:, 0, H:R], acc[:, 0, H:R], act_hi[:, 0, H:R]).then_inc(x_lo_done, 1)
            dve.wait_ge(w_hi_done, 1)
            minus(w_lo[0][:, C:WB], w_stage[:, 0, C:WB], w_hi[0][:, C:WB]).then_inc(w_lo_done, 1)
            split_x(1)
            split_x(2)
            split_w(1, 1)
            split_x(3)
            split_x(4)
            split_w(2, 0)
            split_x(5)
            split_x(6)
            split_x(7)
            split_w(3, 1)
            split_ctxT(0)
            split_ctx(0, 0)
            split_ctx(0, 1)
            split_w(J_GX, 0)

            def copy_q(b):
                nc.vector.tensor_copy(qb_lo[:, :, :], q_lo[:, :, bass.ds(b * N, N)]).then_inc(qb_copied, 1)

            for h in range(2):
                for c in range(KC):
                    dve.wait_ge(q_hi_done, h * KC + c + 1)
                    done = minus(q_lo[:, c, h * H:(h + 1) * H], bank(c + 4 * h, H),
                                 q_hi[:, c, h * H:(h + 1) * H]).then_inc(q_lo_done, 1)
                if h == 0:
                    dve.wait_ge(q_lo_done, KC)
                    copy_q(0)
            dve.wait_ge(q_lo_done, 2 * KC)

            def step(b, slot, more):
                for h in range(2):
                    dve.wait_ge(scores_made, 2 * b + h + 1)
                    nc.vector.reduce_max(top_score[:, h:h + 1], bank(h, MH + 1, N), AX.X).then_inc(top_found, 1)
                dve.wait_ge(top_found, 2 * b + 2)
                nc.vector.tensor_scalar(neg_top[:, :], top_score[:, 0:1], top_score[:, 1:2],
                                        -float(D) ** -0.5, ALU.max, ALU.mult).then_inc(neg_top_set, 1)
                if more:
                    copy_q(b + 1)
                split_w(J_GX + 1 + b, 1 - slot)
                if not isinstance(b, int) or b > 0:
                    split_ctx(b, 1)
                dve.wait_ge(exp_done, b + 1)
                nc.vector.reciprocal(row_inv[:, :], row_sum[:, :]).then_inc(inv_set, 1)
                dve.wait_ge(pt_hi_done, b + 1)
                minus(pt_lo[:, 0:MT, :], bank(PTB, MT * N).rearrange("p (t n) -> p t n", n=N), pt_hi[:, 0:MT, :])
                minus(pt_lo[0:ML, MT, :], bank(PTB5, N, ML, KC * N), pt_hi[0:ML, MT, :]).then_inc(pt_lo_done, 1)
                if more:
                    split_ctxT(b + 1)
                dve.wait_ge(w_used, J_GX + 1 + b)
                nc.vector.tensor_copy(acc[:, bass.ds(b, 1), H:R].rearrange("p k r -> p (k r)"),
                                      bank(GXB + 1, H)).then_inc(gx_saved, 1)
                dve.wait_ge(at_hi_done, b + 1)
                minus(q_lo[:, :, bass.ds(b * N, N)], bank(PTB5, KC * N).rearrange("p (c n) -> p c n", n=N),
                      q_hi[:, :, bass.ds(b * N, N)]).then_inc(at_lo_done, 1)
                if more:
                    split_ctx(b + 1, 0)

            step(0, 0, True)
            step(1, 1, True)
            with dve.Fori(1, B // 2 - 1) as i:
                step(2 * i, 0, True)
                step(2 * i + 1, 1, True)
            step(B - 2, 0, True)
            step(B - 1, 1, False)
            split_w(J_MC + 1, 1)

            dve.wait_ge(mc_made, 1)
            nc.vector.memset(mean_w[:, :], 1.0 / D).then_inc(mean_w_set, 1)
            nc.vector.memset(ones[:, :], 1.0).then_inc(mean_w_set, 1)
            nc.vector.memset(minus_half[:, :], -0.5).then_inc(mean_w_set, 1)
            nc.vector.memset(square_sum[:, :, :], 0.0).then_inc(mean_w_set, 1)

            def mc_tile(k, u):
                dve.wait_ge(mc_saved, k + 1)
                minus(*(a[:, bass.ds(k, 1), :].rearrange("p k r -> p (k r)") for a in (act_lo, mc, act_hi)))\
                    .then_inc(mc_lo_done, 1)

            def mc_pair(q, slot):
                mc_tile(2 * q, 0)
                mc_tile(2 * q + 1, 1)
                split_w(J_MC + 2 + q, slot)

            with dve.Fori(0, KD // 4) as i:
                q = 2 * i
                mc_pair(q, 0)
                mc_pair(q + 1, 1)
            dve.wait_ge(mean_w_set, 4)
            dve.wait_ge(const_in, 32)
            dve.wait_ge(xa_in, 16)

            def sum_squares(t, h, slot):
                dve.wait_ge(squared, t + 1)
                if not isinstance(t, int) or t > 0:
                    dve.wait_ge(summed, t)
                nc.vector.tensor_tensor(square_sum[:, h, :], square_sum[:, h, :], square[:, slot, :],
                                        ALU.add).then_inc(summed, 1)

            def gate_step(t, k, h, slot, more=True, meanwhile=None, part=slice(0, H)):
                rows, mc_rows, xa_rows = (
                    a[:, bass.ds(k, 1), h * H + part.start:h * H + part.stop].rearrange("p k r -> p (k r)")
                    for a in (acc, mc, x_again))
                g = gate[:, slot, part]
                dve.wait_ge(gate_made, t + 1)
                nc.vector.tensor_tensor(g, bank(G2B + slot, part.stop - part.start, P, part.start), rows,
                                        ALU.add).then_inc(gate_summed, 1)
                if meanwhile is not None:
                    meanwhile()
                dve.wait_ge(gate_done, t + 1)
                nc.vector.tensor_tensor(g, g, mc_rows, ALU.mult).then_inc(gated, 1)
                dve.wait_ge(gated, t + 1)
                nc.vector.tensor_tensor(rows, g, xa_rows, ALU.add).then_inc(fused, 1)
                if more:
                    split_w(J_G2 + 2 + t, slot)

            def mean_plus_eps(g):
                b0, n = GROUPS[g]
                dve.wait_ge(mean_made, g + 1)
                nc.vector.tensor_scalar(rms[:, b0:b0 + n], bank(MSB[g], n, N), EPS, None,
                                        ALU.add).then_inc(mean_copied, 1)

            def diagonals(g):
                dve.wait_ge(rooted, g + 1)
                for b in range(GROUPS[g][0], sum(GROUPS[g])):
                    nc.vector.tensor_scalar(rms_diag[:, b, :], ident[:, :], rms[:, b:b + 1], None,
                                            ALU.mult).then_inc(diag_done, 1)

            def output(k, g):
                b0, n = GROUPS[g]
                rows = acc[:, bass.ds(k, 1), b0 * N:(b0 + n) * N].rearrange("p k r -> p (k r)")
                nc.vector.scalar_tensor_tensor(rows, rows, norm_t[:, bass.ds(k, 1)], bank(RIB[g], n * N),
                                               ALU.mult, ALU.mult).then_inc(out_done[g], 1)

            gate_step(0, 0, 0, 0)
            gate_step(1, 1, 0, 1, meanwhile=lambda: sum_squares(0, 0, 0))
            with dve.Fori(1, KD // 2) as i:
                gate_step(2 * i, 2 * i, 0, 0, meanwhile=lambda: sum_squares(2 * i - 1, 0, 1))
                gate_step(2 * i + 1, 2 * i + 1, 0, 1, meanwhile=lambda: sum_squares(2 * i, 0, 0))
            sum_squares(KD - 1, 0, 1)
            mean_plus_eps(0)

            def both(t, h, slot, k):
                sum_squares(t, h, slot)
                output(k, 0)

            gate_step(KD, 0, 1, 0)
            gate_step(KD + 1, 1, 1, 1, meanwhile=lambda: sum_squares(KD, 1, 0))
            dve.wait_ge(inv_made, 1)
            with dve.Fori(KD // 2 + 1, STEPS // 2 - 1) as i:
                gate_step(2 * i, 2 * i - KD, 1, 0, meanwhile=lambda: both(2 * i - 1, 1, 1, 2 * i - KD - 2))
                gate_step(2 * i + 1, 2 * i + 1 - KD, 1, 1, meanwhile=lambda: both(2 * i, 1, 0, 2 * i - KD - 1))
            gate_step(STEPS - 2, KD - 2, 1, 0, False, lambda: both(STEPS - 3, 1, 1, KD - 4))
            output(KD - 3, 0)
            sum_squares(STEPS - 2, 1, 0)
            output(KD - 2, 0)
            gate_step(STEPS - 1, KD - 1, 1, 1, False, lambda: output(KD - 1, 0), slice(0, H // 2))
            gate_step(STEPS, KD - 1, 1, 0, False, None, slice(H // 2, H))
            mean_plus_eps(1)
            diagonals(1)
            mean_plus_eps(2)
            dve.wait_ge(inv_made, 2)
            for k in range(KD // 2):
                output(k, 1)
            diagonals(2)
            for k in range(KD // 2, KD):
                output(k, 1)
            dve.wait_ge(inv_made, 3)
            for k in range(KD):
                output(k, 2)

        @block.gpsimd
        def _(pool):
            nc.gpsimd.memset(ident[:, :], 0.0).then_inc(ident_zeroed, 1)
            pool.wait_ge(ident_zeroed, 1)
            nc.gpsimd.affine_select(out=ident[:, :], in_=ident[:, :], compare_op=ALU.not_equal, fill=1.0,
                                    base=0, pattern=[[-1, N]], channel_multiplier=1).then_inc(consts_set, 1)

            for g, (b0, n) in enumerate(GROUPS):
                pool.wait_ge(mean_copied, g + 1)
                nc.gpsimd.tensor_tensor(rms[:, b0:b0 + n], rms[:, b0:b0 + n], minus_half[:, 0:n],
                                        ALU.pow).then_inc(rooted, 1)
                if g == 0:
                    pool.wait_ge(rooted, 1)
                    for b in range(n):
                        nc.gpsimd.tensor_scalar(rms_diag[:, b, :], ident[:, :], rms[:, b:b + 1], None,
                                                ALU.mult).then_inc(diag_done, 1)


def kernel(x, ctx_1024, L0_xattn_W_mem, L0_xattn_W_gate, L0_xattn_b_gate, L0_xattn_norm_w):
    import numpy as np
    import concourse.bacc as bacc
    from concourse.bass_utils import run_bass_kernel_spmd

    x, ctx, wm, wg = (np.asarray(a) for a in (x, ctx_1024, L0_xattn_W_mem, L0_xattn_W_gate))
    wg = wg.reshape(KD, P, 2, KD, P).transpose(2, 0, 4, 3, 1)
    arrays = {
        "xT": x.reshape(R, D).T,
        "ctxT": ctx.transpose(0, 2, 1),
        "ctxN": ctx,
        "w_mem": wm.reshape(KD // 2, 2, P, C).transpose(0, 2, 1, 3).reshape(KD // 2, P, WB),
        "w_gate_x": wg[0].reshape(KD, P, WB),
        "w_mem_t": wm.reshape(KD // 2, 2, P, KC, P).transpose(0, 4, 1, 3, 2).reshape(KD // 2, P, WB),
        "w_gate_mc": wg[1].reshape(KD, P, WB),
        "b_gate": np.asarray(L0_xattn_b_gate).reshape(KD, P).T,
        "norm_w": np.asarray(L0_xattn_norm_w).reshape(KD, P).T,
    }
    arrays = {k: np.ascontiguousarray(v) for k, v in arrays.items()}
    nc = bacc.Bacc("TRN2", target_bir_lowering=False, num_devices=1)
    args = [nc.dram_tensor(k, v.shape, mybir.dt.from_np(v.dtype), kind="ExternalInput").ap()
            for k, v in arrays.items()]
    out = nc.dram_tensor("outT", (D, R), mybir.dt.float32, kind="ExternalOutput").ap()
    build(nc, *args, out)
    got = run_bass_kernel_spmd(nc, [arrays], core_ids=[0]).results[0]["outT"]
    return np.ascontiguousarray(got.T).reshape(B, N, D)
```

```python
from contextlib import ExitStack

import concourse.bass as bass
from concourse import mybir

B, N, D = 8, 100, 1024
M, C = 722, 512
P = 128
R = B * N
H = R // 2
KD, KC = D // P, C // P
MT = M // P
ML = M - MT * P
MH = M // 2
BANK = 512
WB = KD * P
EPS = 1e-6
WARM_UP = 34
NH = H // N
GROUPS = ((0, NH), (NH, NH // 2), (NH + NH // 2, NH // 2))
SP_STORES = ((0, 0, 2), (0, 2, 4), (0, 4, 6), (0, 6, 8), (1, 0, 2), (1, 4, 6), (2, 0, 2), (2, 4, 6))
ACT_STORES = ((1, 2, 4), (1, 6, 8), (2, 2, 4), (2, 6, 8))

J_MEM = 0
J_GX = J_MEM + KD // 2
J_MC = J_GX + KD
J_G2 = J_MC + KD // 2
STEPS = 2 * KD
PARTS = STEPS + 1


def build(nc, xT, ctxT, ctxN, w_mem, w_gate_x, w_mem_t, w_gate_mc, b_gate, norm_w, outT):
    F32, F32R = mybir.dt.float32, mybir.dt.float32r
    ALU, ACT, AX = mybir.AluOpType, mybir.ActivationFunctionType, mybir.AxisListType

    top = ExitStack()
    with top:
        def sb(scope, name, shape, dt=F32):
            return scope.enter_context(nc.sbuf_tensor(name, shape, dt))

        def sem(name):
            return top.enter_context(nc.semaphore(name))

        act_hi = sb(top, "act_hi", [P, KD, R], F32R)
        act_lo = sb(top, "act_lo", [P, KD, R], F32R)
        q_hi = sb(top, "q_hi", [P, KC, R], F32R)
        q_lo = sb(top, "q_lo", [P, KC, R], F32R)
        acc = sb(top, "acc", [P, KD, R])
        w_stage = sb(top, "w_stage", [P, 2, WB])
        w_hi = [sb(top, f"w_hi{i}", [P, WB], F32R) for i in range(2)]
        w_lo = [sb(top, f"w_lo{i}", [P, WB], F32R) for i in range(2)]
        ident = sb(top, "ident", [N, N])
        bias_t = sb(top, "bias_t", [P, KD])
        norm_t = sb(top, "norm_t", [P, KD])
        table_probe = sb(top, "table_probe", [P, 1])
        idle_work = sb(top, "idle_work", [P, P], mybir.dt.bfloat16)
        top_score = sb(top, "top_score", [N, 2])
        neg_top = sb(top, "neg_top", [N, 1])
        row_sum = sb(top, "row_sum", [N, 1])
        row_inv = sb(top, "row_inv", [N, 1])

        with ExitStack() as attn:
            ct_stage = sb(attn, "ct_stage", [P, KC, M])
            cn_stage = sb(attn, "cn_stage", [P, MT + 1, C])
            ct_hi = sb(attn, "ct_hi", [P, KC, M], F32R)
            ct_lo = sb(attn, "ct_lo", [P, KC, M], F32R)
            cn_hi = sb(attn, "cn_hi", [P, MT + 1, C], F32R)
            cn_lo = sb(attn, "cn_lo", [P, MT + 1, C], F32R)
            qb_hi = sb(attn, "qb_hi", [P, KC, N], F32R)
            qb_lo = sb(attn, "qb_lo", [P, KC, N], F32R)
            probs = sb(attn, "probs", [N, M])
            pt_hi = sb(attn, "pt_hi", [P, MT + 1, N], F32R)
            pt_lo = sb(attn, "pt_lo", [P, MT + 1, N], F32R)
            pc = sb(attn, "pc", [N, C])
        mc = sb(top, "mc", [P, KD, R])
        x_again = sb(top, "x_again", [P, KD, R])
        gate = sb(top, "gate", [P, 2, H])
        square = sb(top, "square", [P, 2, H])
        square_sum = sb(top, "square_sum", [P, 2, H])
        mean_w = sb(top, "mean_w", [P, 1])
        ones = sb(top, "ones", [N, P])
        minus_half = sb(top, "minus_half", [N, B])
        rms = sb(top, "rms", [N, B])
        rms_diag = sb(top, "rms_diag", [N, B, N])

        ps = top.enter_context(nc.psum_tensor("ps", [P, 8 * BANK], F32))

        def bank(i, cols, rows=P, at=0):
            return ps[0:rows, i * BANK + at:i * BANK + at + cols]

        scores = ps[0:N, 0:2 * (BANK + 1)].rearrange("p (h m) -> p h m", h=2)[:, :, 0:MH]
        GXB, PTB, PTB5, PCB = 2, 4, 5, 6
        G2B, MSB, RIB = 4, (6, 2, 1), (7, 3, 0)

        x_in = [sem(f"x_in{k}") for k in range(KD)]
        x_first_in, w_first_in = sem("x_first_in"), [sem(f"w_first_in{i}") for i in range(2)]
        w_in = [sem(f"w_in{s}") for s in range(2)]
        ct_in = [sem(f"ct_in{s}") for s in range(2)]
        cn_in = [sem(f"cn_in{s}") for s in range(2)]
        const_in = sem("const_in")
        xa_in = sem("xa_in")
        stored = sem("stored")
        x_hi_done, x_lo_done = sem("x_hi_done"), sem("x_lo_done")
        w_hi_done, w_lo_done = sem("w_hi_done"), sem("w_lo_done")
        first_hi_done, first_lo_done = sem("first_hi_done"), sem("first_lo_done")
        ct_hi_done, ct_lo_done = sem("ct_hi_done"), sem("ct_lo_done")
        cn_hi_done, cn_lo_done = sem("cn_hi_done"), sem("cn_lo_done")
        q_hi_done, q_lo_done = sem("q_hi_done"), sem("q_lo_done")
        pt_hi_done, pt_lo_done = sem("pt_hi_done"), sem("pt_lo_done")
        at_hi_done, at_lo_done = sem("at_hi_done"), sem("at_lo_done")
        mc_lo_done = sem("mc_lo_done")
        w_used = sem("w_used")
        q_made = sem("q_made")
        scores_made = sem("scores_made")
        probsT_made = sem("probsT_made")
        pc_made = sem("pc_made")
        pcT_made = sem("pcT_made")
        mc_made = sem("mc_made")
        gate_made = sem("gate_made")
        mean_made = sem("mean_made")
        consts_set, idle_work_set = sem("consts_set"), sem("idle_work_set")
        ident_zeroed = sem("ident_zeroed")
        qb_copied = sem("qb_copied")
        top_found, neg_top_set = sem("top_found"), sem("neg_top_set")
        exp_done = sem("exp_done")
        inv_set = sem("inv_set")
        pc_scaled = sem("pc_scaled")
        gx_saved = sem("gx_saved")
        mc_saved = sem("mc_saved")
        gate_summed = sem("gate_summed")
        gate_done = sem("gate_done")
        gated, fused = sem("gated"), sem("fused")
        squared, weighted = sem("squared"), sem("weighted")
        summed = sem("summed")
        mean_copied = sem("mean_copied")
        rooted = sem("rooted")
        diag_done = sem("diag_done")
        inv_made = sem("inv_made")
        mean_w_set = sem("mean_w_set")
        out_done = [sem(f"out_done{g}") for g in range(3)]

        ct_rows = ctxT.rearrange("b c m -> (b c) m")
        cn_rows = ctxN.rearrange("b m c -> (b m) c")
        wgx_rows = w_gate_x.rearrange("t p n -> (t p) n")
        wg2_rows = w_gate_mc.rearrange("t p n -> (t p) n")

        out_v = outT.rearrange("(k p) r -> p k r", p=P)

        def store(eng, g, k, k_end):
            b0, n = GROUPS[g]
            rows = slice(b0 * N, (b0 + n) * N)
            eng.wait_ge(out_done[g], k_end)
            eng.dma_start(out_v[:, k:k_end, rows], acc[:, k:k_end, rows]).then_inc(stored, 16)

        block = top.enter_context(nc.Block())

        @block.sync
        def _(sp):
            def load_x(k):
                sp.dma_start(acc[:, k, :], xT[k * P:(k + 1) * P, :]).then_inc(x_in[k], 16)

            def load_w(j, src, slot):
                if not isinstance(j, int) or j >= 2:
                    sp.wait_ge(w_lo_done, j - 1)
                sp.dma_start(w_stage[:, slot, :], src).then_inc(w_in[slot], 16)

            def load_ctxT(b, first=False):
                for s in range(2):
                    if not first:
                        sp.wait_ge(ct_lo_done, 2 * b - 1 + s)
                    sp.dma_start(ct_stage[:, 2 * s:2 * s + 2, :],
                                 ct_rows[bass.ds(b * C + s * 2 * P, 2 * P), :]
                                 .rearrange("(k p) m -> p k m", p=P)).then_inc(ct_in[s], 16)

            def load_ctx(b, first=False):
                if not first:
                    sp.wait_ge(cn_lo_done, 2 * b - 1)
                sp.dma_start(cn_stage[:, 0:3, :], cn_rows[bass.ds(b * M, 3 * P), :]
                             .rearrange("(t p) c -> p t c", p=P)).then_inc(cn_in[0], 16)
                if not first:
                    sp.wait_ge(cn_lo_done, 2 * b)
                sp.dma_start(cn_stage[:, 3:MT, :], cn_rows[bass.ds(b * M + 3 * P, (MT - 3) * P), :]
                             .rearrange("(t p) c -> p t c", p=P)).then_inc(cn_in[1], 16)
                sp.dma_start(cn_stage[0:ML, MT, :],
                             cn_rows[bass.ds(b * M + MT * P, ML), :]).then_inc(cn_in[1], 16)

            sp.dma_start(acc[:, 0, 0:H], xT[0:P, 0:H]).then_inc(x_first_in, 16)
            for i in range(2):
                cols = slice(i * C // 2, (i + 1) * C // 2)
                sp.dma_start(w_stage[:, 0, cols], w_mem[0][:, cols]).then_inc(w_first_in[i], 16)
            sp.dma_start(acc[:, 0, H:R], xT[0:P, H:R]).then_inc(x_in[0], 16)
            sp.dma_start(w_stage[:, 0, C:WB], w_mem[0][:, C:WB]).then_inc(w_in[0], 16)
            load_x(1)
            load_x(2)
            load_w(1, w_mem[1], 1)
            load_x(3)
            load_x(4)
            load_x(5)
            load_w(2, w_mem[2], 0)
            load_x(6)
            load_x(7)
            load_w(3, w_mem[3], 1)
            load_ctxT(0, first=True)
            load_ctx(0, first=True)
            sp.dma_start(bias_t[:, :], b_gate).then_inc(const_in, 16)
            sp.dma_start(norm_t[:, :], norm_w).then_inc(const_in, 16)
            load_w(J_GX, w_gate_x[0], 0)
            load_w(J_GX + 1, w_gate_x[1], 1)

            def ahead(b, slot):
                load_w(J_GX + 2 + b, wgx_rows[bass.ds((b + 2) * P, P), :], slot)
                load_ctxT(b + 1)
                load_ctx(b + 1)

            with sp.Fori(0, B // 2 - 1) as i:
                b = 2 * i
                ahead(b, 0)
                ahead(b + 1, 1)
            load_w(J_MC, w_mem_t[0], 0)
            load_ctxT(B - 1)
            load_ctx(B - 1)
            load_w(J_MC + 1, w_mem_t[1], 1)
            load_w(J_MC + 2, w_mem_t[2], 0)
            load_w(J_MC + 3, w_mem_t[3], 1)
            load_w(J_G2, w_gate_mc[0], 0)

            sp.wait_ge(mc_made, 1)
            sp.dma_start(x_again[:, :, :], xT.rearrange("(k p) r -> p k r", p=P)).then_inc(xa_in, 16)
            load_w(J_G2 + 1, w_gate_mc[1], 1)
            with sp.Fori(0, KD // 2 - 1) as i:
                for u in range(2):
                    load_w(J_G2 + 2 + 2 * i + u, wg2_rows[bass.ds((2 * i + u + 2) * P, P), :], u)
            with sp.Fori(0, KD // 2) as i:
                for u in range(2):
                    load_w(J_G2 + KD + 2 * i + u, wg2_rows[bass.ds((2 * i + u) * P, P), :], u)
            for args in SP_STORES:
                store(sp, *args)
            sp.wait_ge(stored, 16 * len(SP_STORES + ACT_STORES))

        @block.tensor
        def _(pe):
            def three(outs, weight, stream, first, last):
                (wh, wl), done = weight, None
                for wgt, part in ((wh, 0), (wh, 1), (wl, 0)):
                    for h, o in enumerate(outs):
                        done = nc.tensor.matmul(o, wgt, stream[h][part],
                                                start=first and wgt is wh and part == 0,
                                                stop=last and wgt is wl)
                return done

            def w_tile(slot, i):
                return w_hi[slot][:, i * P:(i + 1) * P], w_lo[slot][:, i * P:(i + 1) * P]

            def halves(hi, lo, k):
                return [(hi[:, k, h * H:(h + 1) * H], lo[:, k, h * H:(h + 1) * H]) for h in range(2)]

            pe.wait_ge(idle_work_set, 1)
            for _ in range(WARM_UP):
                nc.tensor.matmul(bank(7, P), idle_work[:, :], idle_work[:, :], start=True, stop=True)

            for k in range(KD):
                last_k = k == KD - 1
                if k == 0:
                    for h in range(2):
                        if h == 1:
                            pe.wait_ge(x_lo_done, 1)
                        for c in range(KC):
                            if h == 0 and c % 2 == 0:
                                pe.wait_ge(first_lo_done, 2 + c // 2)
                            three([bank(c + 4 * h, H)], w_tile(0, c), halves(act_hi, act_lo, 0)[h:h + 1],
                                  True, False)
                    continue
                if k == 1 or k % 2 == 0:
                    pe.wait_ge(w_lo_done, k // 2 + 1)
                pe.wait_ge(x_lo_done, k + 1)
                if not last_k:
                    for c in range(KC):
                        done = three([bank(c, H), bank(c + 4, H)], w_tile(k // 2 % 2, k % 2 * 4 + c),
                                     halves(act_hi, act_lo, k), False, False)
                else:
                    for h in range(2):
                        for c in range(KC):
                            done = three([bank(c + 4 * h, H)], w_tile(k // 2 % 2, k % 2 * 4 + c),
                                         halves(act_hi, act_lo, k)[h:h + 1], False, True)
                            if (h, c) != (1, KC - 1):
                                done.then_inc(q_made, 1)
                if k % 2 == 1:
                    done.then_inc(w_used, 1)

            def gate_x(slot, k0, k1):
                for k in range(k0, k1):
                    last = three([bank(GXB, H), bank(GXB + 1, H)], w_tile(slot, k),
                                 halves(act_hi, act_lo, k), k == 0, k == KD - 1)
                return last

            def step(b, slot, cuts):
                def fill(i):
                    if cuts[i] < cuts[i + 1]:
                        last = gate_x(slot, cuts[i], cuts[i + 1])
                        if cuts[i + 1] == KD:
                            last.then_inc(w_used, 1)

                if cuts[1] > 0:
                    pe.wait_ge(w_lo_done, J_GX + 1 + b)
                    fill(0)
                pe.wait_ge(ct_lo_done, 2 * b + 2)
                pe.wait_ge(qb_copied, 2 * b + 2)
                for h in range(2):
                    at = h * (MH - 1)
                    for k in range(KC):
                        for lhs, rhs, part in ((qb_hi, ct_hi, 0), (qb_hi, ct_lo, 1), (qb_lo, ct_hi, 2)):
                            done = nc.tensor.matmul(bank(h, MH + 1, N), lhs[:, k, :],
                                                    rhs[:, k, at:at + MH + 1],
                                                    start=k == 0 and part == 0,
                                                    stop=k == KC - 1 and part == 2)
                    done.then_inc(scores_made, 1)
                if cuts[1] == 0:
                    pe.wait_ge(w_lo_done, J_GX + 1 + b)
                    pe.wait_ge(gx_saved, 2 * b)
                fill(1)
                pe.wait_ge(exp_done, b + 1)
                for t in range(MT + 1):
                    rows = P if t < MT else ML
                    o = bank(PTB, N, P, t * N) if t < MT else bank(PTB5, N, ML, KC * N)
                    done = nc.tensor.transpose(o, probs[:, t * P:t * P + rows], ident[:, :])
                done.then_inc(probsT_made, 1)
                fill(2)
                pe.wait_ge(pt_lo_done, b + 1)
                for t in range(MT + 1):
                    if t in (0, 3):
                        pe.wait_ge(cn_lo_done, 2 * b + 1 + t // 3)
                    rows = P if t < MT else ML
                    for lhs, rhs, part in ((pt_hi, cn_hi, 0), (pt_hi, cn_lo, 1), (pt_lo, cn_hi, 2)):
                        done = nc.tensor.matmul(bank(PCB, C, N), lhs[0:rows, t, :], rhs[0:rows, t, :],
                                                start=t == 0 and part == 0, stop=t == MT and part == 2)
                done.then_inc(pc_made, 1)
                fill(3)
                pe.wait_ge(pc_scaled, b + 1)
                for c in range(KC):
                    done = nc.tensor.transpose(bank(PTB5, N, P, c * N), pc[:, c * P:(c + 1) * P],
                                               ident[:, :])
                done.then_inc(pcT_made, 1)

            pe.wait_ge(consts_set, 1)
            pe.wait_ge(q_lo_done, KC)
            step(0, 0, (0, 2, 5, 7, KD))
            CUTS = (0, 0, 4, 7, KD)
            step(1, 1, CUTS)
            with pe.Fori(1, B // 2) as i:
                step(2 * i, 0, CUTS)
                step(2 * i + 1, 1, CUTS)

            def mc_block(q, slot, free, first_tile=0):
                pe.wait_ge(w_lo_done, J_MC + 1 + q)
                for u in range(first_tile, 2):
                    if free:
                        pe.wait_ge(mc_saved, 2 * q + u - 1)
                    for k in range(KC):
                        done = three([bank(2 * u, H), bank(2 * u + 1, H)], w_tile(slot, u * KC + k),
                                     halves(q_hi, q_lo, k), k == 0, k == KC - 1)
                    done.then_inc(mc_made, 1)

            pe.wait_ge(w_lo_done, J_MC + 1)
            for h in range(2):
                pe.wait_ge(at_lo_done, B // 2 if h == 0 else B)
                for k in range(KC):
                    done = three([bank(h, H)], w_tile(0, k), [halves(q_hi, q_lo, k)[h]], k == 0, k == KC - 1)
            done.then_inc(mc_made, 1)
            pe.wait_ge(gx_saved, 2 * B)
            mc_block(0, 0, False, first_tile=1)
            mc_block(1, 1, True)
            mc_block(2, 0, True)
            mc_block(3, 1, True)

            def gate_mc(t, h, slot, first=False, part=slice(0, H), psum=None, between=None):
                if part.start == 0:
                    pe.wait_ge(w_lo_done, J_G2 + 1 + t)
                if not first:
                    pe.wait_ge(gate_summed, t - 1 + (part.start > 0))
                for k in range(KD):
                    if first and slot == 0:
                        pe.wait_ge(mc_lo_done, k + 1)
                    stream = [(act_hi[:, k, h * H + part.start:h * H + part.stop],
                               act_lo[:, k, h * H + part.start:h * H + part.stop])]
                    o = bank(G2B + (slot if psum is None else psum), part.stop - part.start, P, part.start)
                    done = three([o], w_tile(slot, k), stream, k == 0, k == KD - 1)
                    if between is not None and k == between[0]:
                        between[1]()
                done.then_inc(gate_made, 1)

            def mean_square(g, done_sums):
                b0, n = GROUPS[g]
                pe.wait_ge(summed, done_sums)
                for i in range(n):
                    at = (b0 + i) % NH * N
                    done = nc.tensor.matmul(bank(MSB[g], 1, N, i), square_sum[:, b0 // NH, at:at + N],
                                            mean_w[:, :], start=True, stop=True)
                done.then_inc(mean_made, 1)

            def inverse(g):
                b0, n = GROUPS[g]
                pe.wait_ge(diag_done, b0 + n)
                for i in range(n):
                    done = nc.tensor.matmul(bank(RIB[g], N, P, i * N), ones[:, :], rms_diag[:, b0 + i, :],
                                            start=True, stop=True)
                done.then_inc(inv_made, 1)

            gate_mc(0, 0, 0, first=True)
            gate_mc(1, 0, 1, first=True)
            with pe.Fori(1, KD // 2) as i:
                gate_mc(2 * i, 0, 0)
                gate_mc(2 * i + 1, 0, 1)
            gate_mc(KD, 1, 0)
            gate_mc(KD + 1, 1, 1, between=(2, lambda: mean_square(0, KD)))
            gate_mc(KD + 2, 1, 0, between=(2, lambda: inverse(0)))
            gate_mc(KD + 3, 1, 1)
            with pe.Fori(KD // 2 + 2, STEPS // 2 - 1) as i:
                gate_mc(2 * i, 1, 0)
                gate_mc(2 * i + 1, 1, 1)
            gate_mc(STEPS - 2, 1, 0)
            gate_mc(STEPS - 1, 1, 1, part=slice(0, H // 2))
            gate_mc(STEPS - 1, 1, 1, part=slice(H // 2, H), psum=0)
            mean_square(1, STEPS)
            inverse(1)
            mean_square(2, PARTS)
            inverse(2)

        @block.scalar
        def _(act):
            def split_w(j, slot, free=None):
                act.wait_ge(w_in[slot], 8 * (j - slot) + 16)
                if free is not None:
                    act.wait_ge(*free)
                elif not isinstance(j, int) or j >= 2:
                    act.wait_ge(w_used, j - 1)
                nc.scalar.activation(w_hi[slot][:, :], w_stage[:, slot, :], ACT.Copy).then_inc(w_hi_done, 1)

            def split_x(k):
                act.wait_ge(x_in[k], 16)
                nc.scalar.activation(act_hi[:, k, :], acc[:, k, :], ACT.Copy).then_inc(x_hi_done, 1)

            def split_ctxT(b):
                if not isinstance(b, int) or b > 0:
                    act.wait_ge(scores_made, 2 * b)
                for s in range(2):
                    act.wait_ge(ct_in[s], 16 * b + 16)
                    nc.scalar.activation(ct_hi[:, 2 * s:2 * s + 2, :], ct_stage[:, 2 * s:2 * s + 2, :],
                                         ACT.Copy).then_inc(ct_hi_done, 1)

            def split_ctx(b, part):
                if part == 0:
                    if not isinstance(b, int) or b > 0:
                        act.wait_ge(pc_made, b)
                    act.wait_ge(cn_in[0], 16 * b + 16)
                    nc.scalar.activation(cn_hi[:, 0:3, :], cn_stage[:, 0:3, :], ACT.Copy).then_inc(cn_hi_done, 1)
                else:
                    act.wait_ge(cn_in[1], 32 * b + 32)
                    nc.scalar.activation(cn_hi[:, 3:MT, :], cn_stage[:, 3:MT, :], ACT.Copy)
                    nc.scalar.activation(cn_hi[0:ML, MT, :], cn_stage[0:ML, MT, :],
                                         ACT.Copy).then_inc(cn_hi_done, 1)

            act.wait_ge(x_first_in, 16)
            nc.scalar.activation(act_hi[:, 0, 0:H], acc[:, 0, 0:H], ACT.Copy).then_inc(first_hi_done, 1)
            for i in range(2):
                cols = slice(i * C // 2, (i + 1) * C // 2)
                act.wait_ge(w_first_in[i], 16)
                nc.scalar.activation(w_hi[0][:, cols], w_stage[:, 0, cols], ACT.Copy).then_inc(first_hi_done, 1)
            act.wait_ge(x_in[0], 16)
            nc.scalar.activation(act_hi[:, 0, H:R], acc[:, 0, H:R], ACT.Copy).then_inc(x_hi_done, 1)
            act.wait_ge(w_in[0], 16)
            nc.scalar.activation(w_hi[0][:, C:WB], w_stage[:, 0, C:WB], ACT.Copy).then_inc(w_hi_done, 1)
            split_x(1)
            split_x(2)
            split_w(1, 1)
            split_x(3)
            split_x(4)
            split_w(2, 0)
            split_x(5)
            split_x(6)
            split_x(7)
            split_w(3, 1)
            split_ctxT(0)
            split_ctx(0, 0)
            split_ctx(0, 1)
            split_w(J_GX, 0)

            def copy_q(b):
                nc.scalar.activation(qb_hi[:, :, :], q_hi[:, :, bass.ds(b * N, N)].bitcast(F32),
                                     ACT.Copy).then_inc(qb_copied, 1)

            for h in range(2):
                for c in range(KC):
                    if (h, c) != (1, KC - 1):
                        act.wait_ge(q_made, h * KC + c + 1)
                    else:
                        act.wait_ge(w_used, KD // 2)
                    nc.scalar.activation(q_hi[:, c, h * H:(h + 1) * H], bank(c + 4 * h, H),
                                         ACT.Copy).then_inc(q_hi_done, 1)
                if h == 0:
                    act.wait_ge(q_hi_done, KC)
                    copy_q(0)
            act.wait_ge(q_hi_done, 2 * KC)

            def save_gate(b):
                nc.scalar.activation(acc[:, bass.ds(b, 1), 0:H].rearrange("p k r -> p (k r)"), bank(GXB, H),
                                     ACT.Copy).then_inc(gx_saved, 1)

            def step(b, slot, more):
                act.wait_ge(neg_top_set, b + 1)
                nc.scalar.activation(probs[:, :].rearrange("p (h m) -> p h m", h=2), scores, ACT.Exp,
                                     bias=neg_top[:, :], scale=float(D) ** -0.5,
                                     accum_out=row_sum[:, :]).then_inc(exp_done, 1)
                split_w(J_GX + 1 + b, 1 - slot)
                if not isinstance(b, int) or b > 0:
                    split_ctx(b, 1)
                if more:
                    copy_q(b + 1)
                act.wait_ge(probsT_made, b + 1)
                nc.scalar.activation(pt_hi[:, 0:MT, :], bank(PTB, MT * N).rearrange("p (t n) -> p t n", n=N),
                                     ACT.Copy)
                nc.scalar.activation(pt_hi[0:ML, MT, :], bank(PTB5, N, ML, KC * N), ACT.Copy).then_inc(pt_hi_done, 1)
                if more:
                    split_ctxT(b + 1)
                act.wait_ge(pc_made, b + 1)
                act.wait_ge(inv_set, b + 1)
                nc.scalar.activation(pc[:, :], bank(PCB, C, N), ACT.Copy,
                                     scale=row_inv[:, :]).then_inc(pc_scaled, 1)
                act.wait_ge(pcT_made, b + 1)
                if more:
                    save_gate(b)
                nc.scalar.activation(q_hi[:, :, bass.ds(b * N, N)],
                                     bank(PTB5, KC * N).rearrange("p (c n) -> p c n", n=N),
                                     ACT.Copy).then_inc(at_hi_done, 1)
                if not more:
                    act.wait_ge(w_used, J_GX + 1 + b)
                    save_gate(b)
                if more:
                    split_ctx(b + 1, 0)

            step(0, 0, True)
            step(1, 1, True)
            with act.Fori(1, B // 2 - 1) as i:
                step(2 * i, 0, True)
                step(2 * i + 1, 1, True)
            step(B - 2, 0, True)
            step(B - 1, 1, False)
            split_w(J_MC + 1, 1)

            act.wait_ge(const_in, 32)
            nc.scalar.activation(table_probe[:, :], bias_t[:, 0:1], ACT.Sigmoid)

            def mc_tile(k, u):
                act.wait_ge(mc_made, k + 1)
                src = ps[:, 2 * u * BANK:(2 * u + 2) * BANK].rearrange("p (h m) -> p h m", h=2)[:, :, 0:H]
                nc.scalar.activation(act_hi[:, bass.ds(k, 1), :].rearrange("p k (h r) -> p (k h) r", h=2), src,
                                     ACT.Copy)
                nc.scalar.activation(mc[:, bass.ds(k, 1), :].rearrange("p k (h r) -> p (k h) r", h=2), src,
                                     ACT.Copy).then_inc(mc_saved, 1)

            def mc_pair(q, slot):
                mc_tile(2 * q, 0)
                mc_tile(2 * q + 1, 1)
                split_w(J_MC + 2 + q, slot, (mc_made, 2 * q + 2))

            with act.Fori(0, KD // 4) as i:
                q = 2 * i
                mc_pair(q, 0)
                mc_pair(q + 1, 1)

            def sigmoid(t, k, slot, part=slice(0, H)):
                act.wait_ge(gate_summed, t + 1)
                nc.scalar.activation(gate[:, slot, part], gate[:, slot, part], ACT.Sigmoid,
                                     bias=bias_t[:, bass.ds(k, 1)]).then_inc(gate_done, 1)

            def finish(t, k, h, slot, part=slice(0, H), between=None):
                act.wait_ge(fused, t + 1)
                if not isinstance(t, int) or t >= 2:
                    act.wait_ge(summed, t - 1)
                rows = acc[:, bass.ds(k, 1), h * H + part.start:h * H + part.stop].rearrange("p k r -> p (k r)")
                nc.scalar.activation(square[:, slot, part], rows, ACT.Square).then_inc(squared, 1)
                if between is not None:
                    between()
                act.wait_ge(squared, t + 1)
                nc.scalar.activation(rows, rows, ACT.Copy, scale=norm_t[:, bass.ds(k, 1)]).then_inc(weighted, 1)

            def gate_step(t, k, h, slot, first=False):
                split_w(J_G2 + 2 + t, slot, (gate_made, t + 1))
                sigmoid(t, k, slot)
                if not first:
                    finish(t - 1, k - 1, h, 1 - slot)

            gate_step(0, 0, 0, 0, first=True)
            gate_step(1, 1, 0, 1)
            with act.Fori(1, KD // 2) as i:
                gate_step(2 * i, 2 * i, 0, 0)
                gate_step(2 * i + 1, 2 * i + 1, 0, 1)
            finish(KD - 1, KD - 1, 0, 1)
            gate_step(KD, 0, 1, 0, first=True)
            gate_step(KD + 1, 1, 1, 1)
            with act.Fori(KD // 2 + 1, STEPS // 2 - 1) as i:
                gate_step(2 * i, 2 * i - KD, 1, 0)
                gate_step(2 * i + 1, 2 * i + 1 - KD, 1, 1)
            finish(STEPS - 3, KD - 3, 1, 1)
            sigmoid(STEPS - 2, KD - 2, 0)
            finish(STEPS - 2, KD - 2, 1, 0,
                   between=lambda: sigmoid(STEPS - 1, KD - 1, 1, slice(0, H // 2)))
            finish(STEPS - 1, KD - 1, 1, 1, slice(0, H // 2),
                   between=lambda: sigmoid(STEPS, KD - 1, 0, slice(H // 2, H)))
            finish(STEPS, KD - 1, 1, 0, slice(H // 2, H))
            for args in ACT_STORES:
                store(act, *args)

        @block.vector
        def _(dve):
            def minus(out, whole, hi):
                return nc.vector.tensor_tensor(out, whole, hi.bitcast(F32), ALU.subtract)

            def split_w(j, slot):
                dve.wait_ge(w_hi_done, j + 1)
                minus(w_lo[slot][:, :], w_stage[:, slot, :], w_hi[slot][:, :]).then_inc(w_lo_done, 1)

            def split_x(k):
                dve.wait_ge(x_hi_done, k + 1)
                minus(act_lo[:, k, :], acc[:, k, :], act_hi[:, k, :]).then_inc(x_lo_done, 1)

            def split_ctxT(b):
                for s in range(2):
                    dve.wait_ge(ct_hi_done, 2 * b + s + 1)
                    minus(ct_lo[:, 2 * s:2 * s + 2, :], ct_stage[:, 2 * s:2 * s + 2, :],
                          ct_hi[:, 2 * s:2 * s + 2, :]).then_inc(ct_lo_done, 1)

            def split_ctx(b, part):
                dve.wait_ge(cn_hi_done, 2 * b + part + 1)
                if part == 0:
                    minus(cn_lo[:, 0:3, :], cn_stage[:, 0:3, :], cn_hi[:, 0:3, :]).then_inc(cn_lo_done, 1)
                else:
                    minus(cn_lo[:, 3:MT, :], cn_stage[:, 3:MT, :], cn_hi[:, 3:MT, :])
                    minus(cn_lo[0:ML, MT, :], cn_stage[0:ML, MT, :], cn_hi[0:ML, MT, :]).then_inc(cn_lo_done, 1)

            nc.vector.memset(idle_work[:, :], 0.0).then_inc(idle_work_set, 1)
            dve.wait_ge(first_hi_done, 1)
            minus(act_lo[:, 0, 0:H], acc[:, 0, 0:H], act_hi[:, 0, 0:H]).then_inc(first_lo_done, 1)
            for i in range(2):
                cols = slice(i * C // 2, (i + 1) * C // 2)
                dve.wait_ge(first_hi_done, i + 2)
                minus(w_lo[0][:, cols], w_stage[:, 0, cols], w_hi[0][:, cols]).then_inc(first_lo_done, 1)
            dve.wait_ge(x_hi_done, 1)
            minus(act_lo[:, 0, H:R], acc[:, 0, H:R], act_hi[:, 0, H:R]).then_inc(x_lo_done, 1)
            dve.wait_ge(w_hi_done, 1)
            minus(w_lo[0][:, C:WB], w_stage[:, 0, C:WB], w_hi[0][:, C:WB]).then_inc(w_lo_done, 1)
            split_x(1)
            split_x(2)
            split_w(1, 1)
            split_x(3)
            split_x(4)
            split_w(2, 0)
            split_x(5)
            split_x(6)
            split_x(7)
            split_w(3, 1)
            split_ctxT(0)
            split_ctx(0, 0)
            split_ctx(0, 1)
            split_w(J_GX, 0)

            def copy_q(b):
                nc.vector.tensor_copy(qb_lo[:, :, :], q_lo[:, :, bass.ds(b * N, N)]).then_inc(qb_copied, 1)

            for h in range(2):
                for c in range(KC):
                    dve.wait_ge(q_hi_done, h * KC + c + 1)
                    done = minus(q_lo[:, c, h * H:(h + 1) * H], bank(c + 4 * h, H),
                                 q_hi[:, c, h * H:(h + 1) * H]).then_inc(q_lo_done, 1)
                if h == 0:
                    dve.wait_ge(q_lo_done, KC)
                    copy_q(0)
            dve.wait_ge(q_lo_done, 2 * KC)

            def save_gate(b):
                dve.wait_ge(w_used, J_GX + 1 + b)
                nc.vector.tensor_copy(acc[:, bass.ds(b, 1), H:R].rearrange("p k r -> p (k r)"),
                                      bank(GXB + 1, H)).then_inc(gx_saved, 1)

            def step(b, slot, more):
                for h in range(2):
                    dve.wait_ge(scores_made, 2 * b + h + 1)
                    nc.vector.reduce_max(top_score[:, h:h + 1], bank(h, MH + 1, N), AX.X).then_inc(top_found, 1)
                dve.wait_ge(top_found, 2 * b + 2)
                nc.vector.tensor_scalar(neg_top[:, :], top_score[:, 0:1], top_score[:, 1:2],
                                        -float(D) ** -0.5, ALU.max, ALU.mult).then_inc(neg_top_set, 1)
                if more:
                    copy_q(b + 1)
                split_w(J_GX + 1 + b, 1 - slot)
                dve.wait_ge(exp_done, b + 1)
                nc.vector.reciprocal(row_inv[:, :], row_sum[:, :]).then_inc(inv_set, 1)
                dve.wait_ge(pt_hi_done, b + 1)
                minus(pt_lo[:, 0:MT, :], bank(PTB, MT * N).rearrange("p (t n) -> p t n", n=N), pt_hi[:, 0:MT, :])
                minus(pt_lo[0:ML, MT, :], bank(PTB5, N, ML, KC * N), pt_hi[0:ML, MT, :]).then_inc(pt_lo_done, 1)
                if not isinstance(b, int) or b > 0:
                    split_ctx(b, 1)
                if more:
                    split_ctxT(b + 1)
                if more:
                    save_gate(b)
                dve.wait_ge(at_hi_done, b + 1)
                minus(q_lo[:, :, bass.ds(b * N, N)], bank(PTB5, KC * N).rearrange("p (c n) -> p c n", n=N),
                      q_hi[:, :, bass.ds(b * N, N)]).then_inc(at_lo_done, 1)
                if not more:
                    save_gate(b)
                if more:
                    split_ctx(b + 1, 0)

            step(0, 0, True)
            step(1, 1, True)
            with dve.Fori(1, B // 2 - 1) as i:
                step(2 * i, 0, True)
                step(2 * i + 1, 1, True)
            step(B - 2, 0, True)
            step(B - 1, 1, False)
            split_w(J_MC + 1, 1)

            dve.wait_ge(mc_made, 1)
            nc.vector.memset(mean_w[:, :], 1.0 / D).then_inc(mean_w_set, 1)
            nc.vector.memset(ones[:, :], 1.0).then_inc(mean_w_set, 1)
            nc.vector.memset(minus_half[:, :], -0.5).then_inc(mean_w_set, 1)
            nc.vector.memset(square_sum[:, :, :], 0.0).then_inc(mean_w_set, 1)

            def mc_tile(k, u):
                dve.wait_ge(mc_saved, k + 1)
                minus(*(a[:, bass.ds(k, 1), :].rearrange("p k r -> p (k r)") for a in (act_lo, mc, act_hi)))\
                    .then_inc(mc_lo_done, 1)

            def mc_pair(q, slot):
                mc_tile(2 * q, 0)
                mc_tile(2 * q + 1, 1)
                split_w(J_MC + 2 + q, slot)

            with dve.Fori(0, KD // 4) as i:
                q = 2 * i
                mc_pair(q, 0)
                mc_pair(q + 1, 1)
            dve.wait_ge(mean_w_set, 4)
            dve.wait_ge(xa_in, 16)

            def sum_squares(t, h, slot, part=slice(0, H)):
                dve.wait_ge(squared, t + 1)
                if not isinstance(t, int) or t > 0:
                    dve.wait_ge(summed, t)
                nc.vector.tensor_tensor(square_sum[:, h, part], square_sum[:, h, part], square[:, slot, part],
                                        ALU.add).then_inc(summed, 1)

            def gate_step(t, k, h, slot, more=True, meanwhile=(), then=(), part=slice(0, H)):
                rows, mc_rows, xa_rows = (
                    a[:, bass.ds(k, 1), h * H + part.start:h * H + part.stop].rearrange("p k r -> p (k r)")
                    for a in (acc, mc, x_again))
                g = gate[:, slot, part]
                dve.wait_ge(gate_made, t + 1)
                nc.vector.tensor_tensor(g, bank(G2B + slot, part.stop - part.start, P, part.start), rows,
                                        ALU.add).then_inc(gate_summed, 1)
                for work in meanwhile:
                    work()
                if more:
                    split_w(J_G2 + 2 + t, slot)
                dve.wait_ge(gate_done, t + 1)
                nc.vector.tensor_tensor(g, g, mc_rows, ALU.mult).then_inc(gated, 1)
                for work in then:
                    work()
                dve.wait_ge(gated, t + 1)
                nc.vector.tensor_tensor(rows, g, xa_rows, ALU.add).then_inc(fused, 1)

            def mean_plus_eps(g):
                b0, n = GROUPS[g]
                dve.wait_ge(mean_made, g + 1)
                nc.vector.tensor_scalar(rms[:, b0:b0 + n], bank(MSB[g], n, N), EPS, None,
                                        ALU.add).then_inc(mean_copied, 1)

            def diagonals(g):
                dve.wait_ge(rooted, g + 1)
                for b in range(GROUPS[g][0], sum(GROUPS[g])):
                    nc.vector.tensor_scalar(rms_diag[:, b, :], ident[:, :], rms[:, b:b + 1], None,
                                            ALU.mult).then_inc(diag_done, 1)

            def output(k, n_tiles, g):
                b0, n = GROUPS[g]
                rows = acc[:, bass.ds(k, n_tiles), b0 * N:(b0 + n) * N]
                inv = bank(RIB[g], n * N).rearrange("p (o r) -> p o r", o=1).to_broadcast([P, n_tiles, n * N])
                nc.vector.tensor_tensor(rows, rows, inv, ALU.mult).then_inc(out_done[g], n_tiles)

            gate_step(0, 0, 0, 0)
            gate_step(1, 1, 0, 1, then=[lambda: sum_squares(0, 0, 0)])
            with dve.Fori(1, KD // 2) as i:
                gate_step(2 * i, 2 * i, 0, 0, then=[lambda: sum_squares(2 * i - 1, 0, 1)])
                gate_step(2 * i + 1, 2 * i + 1, 0, 1, then=[lambda: sum_squares(2 * i, 0, 0)])
            sum_squares(KD - 1, 0, 1)

            gate_step(KD, 0, 1, 0, meanwhile=[lambda: mean_plus_eps(0)])
            gate_step(KD + 1, 1, 1, 1, then=[lambda: sum_squares(KD, 1, 0)])
            dve.wait_ge(weighted, KD)
            dve.wait_ge(inv_made, 1)
            with dve.Fori(KD // 2 + 1, STEPS // 2 - 1) as i:
                gate_step(2 * i, 2 * i - KD, 1, 0, meanwhile=[lambda: output(2 * i - KD - 2, 1, 0)],
                          then=[lambda: sum_squares(2 * i - 1, 1, 1)])
                gate_step(2 * i + 1, 2 * i + 1 - KD, 1, 1, meanwhile=[lambda: output(2 * i - KD - 1, 1, 0)],
                          then=[lambda: sum_squares(2 * i, 1, 0)])
            gate_step(STEPS - 2, KD - 2, 1, 0, False,
                      [lambda: sum_squares(STEPS - 3, 1, 1), lambda: output(KD - 4, 1, 0)])
            gate_step(STEPS - 1, KD - 1, 1, 1, False,
                      [lambda: sum_squares(STEPS - 2, 1, 0)], part=slice(0, H // 2))

            def between():
                output(KD - 2, 1, 0)
                mean_plus_eps(1)

            output(KD - 3, 1, 0)
            sum_squares(STEPS - 1, 1, 1, slice(0, H // 2))
            gate_step(STEPS, KD - 1, 1, 0, False, [between], part=slice(H // 2, H))
            diagonals(1)
            sum_squares(STEPS, 1, 0, slice(H // 2, H))
            output(KD - 1, 1, 0)
            dve.wait_ge(weighted, STEPS)
            dve.wait_ge(inv_made, 2)
            output(0, 2, 1)
            mean_plus_eps(2)
            output(2, 2, 1)
            diagonals(2)
            output(4, 2, 1)
            output(6, 2, 1)
            dve.wait_ge(weighted, PARTS)
            dve.wait_ge(inv_made, 3)
            for k in range(0, KD, 2):
                output(k, 2, 2)

        @block.gpsimd
        def _(pool):
            nc.gpsimd.memset(ident[:, :], 0.0).then_inc(ident_zeroed, 1)
            pool.wait_ge(ident_zeroed, 1)
            nc.gpsimd.affine_select(out=ident[:, :], in_=ident[:, :], compare_op=ALU.not_equal, fill=1.0,
                                    base=0, pattern=[[-1, N]], channel_multiplier=1).then_inc(consts_set, 1)

            for g, (b0, n) in enumerate(GROUPS):
                pool.wait_ge(mean_copied, g + 1)
                nc.gpsimd.tensor_tensor(rms[:, b0:b0 + n], rms[:, b0:b0 + n], minus_half[:, 0:n],
                                        ALU.pow).then_inc(rooted, 1)
                if g == 0:
                    pool.wait_ge(rooted, 1)
                    for b in range(n):
                        nc.gpsimd.tensor_scalar(rms_diag[:, b, :], ident[:, :], rms[:, b:b + 1], None,
                                                ALU.mult).then_inc(diag_done, 1)


def kernel(x, ctx_1024, L0_xattn_W_mem, L0_xattn_W_gate, L0_xattn_b_gate, L0_xattn_norm_w):
    import numpy as np
    import concourse.bacc as bacc
    from concourse.bass_utils import run_bass_kernel_spmd

    x, ctx, wm, wg = (np.asarray(a) for a in (x, ctx_1024, L0_xattn_W_mem, L0_xattn_W_gate))
    wg = wg.reshape(KD, P, 2, KD, P).transpose(2, 0, 4, 3, 1)
    arrays = {
        "xT": x.reshape(R, D).T,
        "ctxT": ctx.transpose(0, 2, 1),
        "ctxN": ctx,
        "w_mem": wm.reshape(KD // 2, 2, P, C).transpose(0, 2, 1, 3).reshape(KD // 2, P, WB),
        "w_gate_x": wg[0].reshape(KD, P, WB),
        "w_mem_t": wm.reshape(KD // 2, 2, P, KC, P).transpose(0, 4, 1, 3, 2).reshape(KD // 2, P, WB),
        "w_gate_mc": wg[1].reshape(KD, P, WB),
        "b_gate": np.asarray(L0_xattn_b_gate).reshape(KD, P).T,
        "norm_w": np.asarray(L0_xattn_norm_w).reshape(KD, P).T,
    }
    arrays = {k: np.ascontiguousarray(v) for k, v in arrays.items()}
    nc = bacc.Bacc("TRN2", target_bir_lowering=False, num_devices=1)
    args = [nc.dram_tensor(k, v.shape, mybir.dt.from_np(v.dtype), kind="ExternalInput").ap()
            for k, v in arrays.items()]
    out = nc.dram_tensor("outT", (D, R), mybir.dt.float32, kind="ExternalOutput").ap()
    build(nc, *args, out)
    got = run_bass_kernel_spmd(nc, [arrays], core_ids=[0]).results[0]["outT"]
    return np.ascontiguousarray(got.T).reshape(B, N, D)
```
